# Optimizing a Trainium2 kernel written in Bass

```python
import numpy as np
import jax
import jax.numpy as jnp

def _softmax(x, axis=-1):
    return jax.nn.softmax(x, axis=axis)
def _gelu(x):
    return jax.nn.gelu(x, approximate=True)
def _silu(x):
    return jax.nn.silu(x)
def _sigmoid(x):
    return jax.nn.sigmoid(x)
def _layernorm(x, axis=-1, eps=1e-5):
    m = jnp.mean(x, axis=axis, keepdims=True)
    v = jnp.var(x, axis=axis, keepdims=True)
    return (x - m) / jnp.sqrt(v + eps)
def _scatter_add(tgt, idx, src, axis=0):
    return tgt.at[idx].add(src)
def _segment_sum(src, seg, n):
    return jax.ops.segment_sum(src, seg, n)

kernel_name = 'mk_conv_seq_d1_conv_nhwc128_f384e9'

def setup_inputs(seed: int = 0):
    np.random.seed(seed)
    _w = jnp.asarray
    def _rec_inputs():
        import jax
        import jax.numpy as jnp
        _gk = jax.random.key(seed)
        x = -0.000125 + 0.9999 * jax.random.normal(jax.random.fold_in(_gk, 1), (1, 512, 512, 128), jnp.float32)
        return x
    x = _rec_inputs()
    def _L0_conv_setup():
        import jax, jax.numpy as jnp
        import numpy as np
        B, N, D = (1, 512, 128)
        LN_EPS = 1e-05
        key = jax.random.key(seed)
        ks = jax.random.split(key, 9)
        s = 1.0 / np.sqrt(D)
        return {'pair_rep': jax.random.normal(ks[0], (B, N, N, D), dtype=jnp.float32), 'Wa': jax.random.normal(ks[1], (D, D), dtype=jnp.float32) * s, 'ba': jnp.zeros((D,), dtype=jnp.float32), 'Wb': jax.random.normal(ks[2], (D, D), dtype=jnp.float32) * s, 'bb': jnp.zeros((D,), dtype=jnp.float32), 'Wg': jax.random.normal(ks[3], (D, D), dtype=jnp.float32) * s, 'bg': jnp.zeros((D,), dtype=jnp.float32), 'Wo': jax.random.normal(ks[4], (D, D), dtype=jnp.float32) * s, 'bo': jnp.zeros((D,), dtype=jnp.float32), 'gamma': jnp.ones((D,), dtype=jnp.float32), 'beta': jnp.zeros((D,), dtype=jnp.float32)}
    _L0_conv_all = _L0_conv_setup()
    _L0_conv_in = {k: v for k, v in _L0_conv_all.items() if k in ('Wa', 'ba', 'Wb', 'bb', 'Wg', 'bg', 'Wo', 'bo', 'gamma', 'beta', )}
    del _L0_conv_all

    return {
        "x": x,
        "L0_conv_Wa": _L0_conv_in["Wa"],
        "L0_conv_ba": _L0_conv_in["ba"],
        "L0_conv_Wb": _L0_conv_in["Wb"],
        "L0_conv_bb": _L0_conv_in["bb"],
        "L0_conv_Wg": _L0_conv_in["Wg"],
        "L0_conv_bg": _L0_conv_in["bg"],
        "L0_conv_Wo": _L0_conv_in["Wo"],
        "L0_conv_bo": _L0_conv_in["bo"],
        "L0_conv_gamma": _L0_conv_in["gamma"],
        "L0_conv_beta": _L0_conv_in["beta"],
    }

def reference(x, L0_conv_Wa, L0_conv_ba, L0_conv_Wb, L0_conv_bb, L0_conv_Wg, L0_conv_bg, L0_conv_Wo, L0_conv_bo, L0_conv_gamma, L0_conv_beta):
    import jax
    import jax.numpy as jnp
    def _L0_conv_ref(pair_rep, Wa, ba, Wb, bb, Wg, bg, Wo, bo, gamma, beta):
        import jax, jax.numpy as jnp
        import numpy as np
        B, N, D = (1, 512, 128)
        LN_EPS = 1e-05
        a = pair_rep @ Wa + ba
        b = pair_rep @ Wb + bb
        g = jax.nn.sigmoid(pair_rep @ Wg + bg)
        update = jnp.einsum('bjic,bjkc->bikc', a, b)
        update = g * update
        update = update @ Wo + bo
        x = pair_rep + update
        mu = jnp.mean(x, axis=-1, keepdims=True)
        var = jnp.mean(jnp.square(x - mu), axis=-1, keepdims=True)
        return (x - mu) * jax.lax.rsqrt(var + LN_EPS) * gamma + beta

    def _gn(v, G=32, eps=1e-5):
        B_, H_, W_, C_ = v.shape
        g = v.reshape(B_, H_, W_, G, C_ // G)
        m = jnp.mean(g, axis=(1, 2, 4), keepdims=True)
        s = jnp.var(g, axis=(1, 2, 4), keepdims=True)
        return ((g - m) / jnp.sqrt(s + eps)).reshape(v.shape)

    def _ln_c(v, eps=1e-6):
        m = jnp.mean(v, axis=-1, keepdims=True)
        s = jnp.var(v, axis=-1, keepdims=True)
        return (v - m) / jnp.sqrt(s + eps)

    def _ln_t(v, eps=1e-5):
        m = jnp.mean(v, axis=-1, keepdims=True)
        s = jnp.var(v, axis=-1, keepdims=True)
        return (v - m) / jnp.sqrt(s + eps)

    def _to_tokens(v):
        B_, H_, W_, C_ = v.shape
        return v.reshape(B_, H_ * W_, C_)
    def _from_tokens(t, like):
        return t.reshape(like.shape)

    x = _L0_conv_ref(x, L0_conv_Wa, L0_conv_ba, L0_conv_Wb, L0_conv_bb, L0_conv_Wg, L0_conv_bg, L0_conv_Wo, L0_conv_bo, L0_conv_gamma, L0_conv_beta)
    return x


_drawn_inputs = setup_inputs


def setup_inputs(seed=0):
    import zlib

    import numpy as np

    out = dict(_drawn_inputs(seed))
    spreads = {'L0_conv_ba': (0.0, 0.1),
     'L0_conv_bb': (0.0, 0.1),
     'L0_conv_bg': (0.0, 0.1),
     'L0_conv_bo': (0.0, 0.8),
     'L0_conv_gamma': (1.0, 0.2),
     'L0_conv_beta': (0.0, 0.1)}
    factors = {}
    for name, (base, spread) in spreads.items():
        noise = np.random.default_rng([zlib.crc32(name.encode()), seed]).standard_normal(out[name].shape)
        drawn = base * np.exp(spread * noise) if base else spread * noise
        out[name] = jnp.asarray(drawn.astype(out[name].dtype))
    for name, factor in factors.items():
        out[name] = (out[name] * factor).astype(out[name].dtype)
    return out
```

```python
from contextlib import ExitStack

import numpy as np
import concourse.bass as bass
from concourse import mybir
from concourse.alu_op_type import AluOpType as ALU

F32 = mybir.dt.float32
F32R = mybir.dt.float32r
BF16 = mybir.dt.bfloat16
ACT = mybir.ActivationFunctionType

P = 128
N = 512
ROW_TILES = N // P
COL_BLOCK = 64
COL_BLOCKS = N // COL_BLOCK
UNITS = COL_BLOCKS * ROW_TILES
CHUNK_COLS = 16
QUARTERS = COL_BLOCK // CHUNK_COLS
CHUNK = CHUNK_COLS * P
CHUNKS = N * N // CHUNK
GROUP = 4
GROUPS = P // GROUP
RUN = GROUP * COL_BLOCK
PAD = 1024
EPS = 1e-5


def project(nc, xT, Wa, Wb, ba, bb, ab_scratch):
    PSUM_SLOTS = 4
    GCOLS = 4
    STEPS = COL_BLOCK // GCOLS
    QSTEPS = STEPS // QUARTERS
    with ExitStack() as ctx:
        sb = lambda name, shape, dt=F32: ctx.enter_context(nc.sbuf_tensor(name, shape, dt))
        sem = lambda name: ctx.enter_context(nc.semaphore(name))
        w_ab = sb("w_ab", [P, 2 * P])
        bias_ab = sb("bias_ab", [P, 2 * P])
        x_tile = sb("x_tile", [P, QUARTERS, CHUNK_COLS, P])
        stage = sb("stage", [P, 2, 2 * P, COL_BLOCK])
        ps = ctx.enter_context(nc.psum_tensor("ps_ab", [P, PSUM_SLOTS, GCOLS, 2 * P], F32))
        weights_in = sem("p1_weights_in")
        bias_in = sem("p1_bias_in")
        x_in = [sem(f"p1_x_in{q}") for q in range(QUARTERS)]
        products = sem("p1_products")
        staged = sem("p1_staged")
        stored = [sem(f"p1_stored{s}") for s in range(2)]
        block = ctx.enter_context(nc.Block())

        @block.sync
        def _(sp):
            sp.dma_start(w_ab[:, 0:P], Wa).then_inc(weights_in, 16)
            sp.dma_start(w_ab[:, P:2 * P], Wb).then_inc(weights_in, 16)
            sp.dma_start(bias_ab[:, 0:P], ba[None, :].to_broadcast([P, P])).then_inc(bias_in, 16)
            sp.dma_start(bias_ab[:, P:2 * P], bb[None, :].to_broadcast([P, P])).then_inc(bias_in, 16)

            def store(cb, jt, unit):
                sp.wait_ge(staged, STEPS * (unit + 1))
                for ab in range(2):
                    sp.dma_start(
                        ab_scratch[:, ab, cb, jt, :, :].rearrange("g p f -> p g f"),
                        stage[:, jt % 2, ab * P:(ab + 1) * P, :].rearrange("p (g c) i -> p g (c i)", c=GROUP),
                    ).then_inc(stored[jt % 2], 16)

            def unit_step(cb, jt, first):
                unit = cb * ROW_TILES + jt
                for q in range(QUARTERS):
                    if not first:
                        sp.wait_ge(products, STEPS * (unit - 1) + QSTEPS * (q + 1))
                    sp.dma_start(x_tile[:, q, :, :].rearrange("p a b -> p (a b)"),
                                 xT[cb * QUARTERS + (jt * (N // CHUNK_COLS) + q), :, :]).then_inc(x_in[q], 16)
                if not first:
                    if jt:
                        store(cb, jt - 1, unit - 1)
                    else:
                        store(cb - 1, ROW_TILES - 1, unit - 1)

            for jt in range(ROW_TILES):
                unit_step(0, jt, jt == 0)
            with sp.Fori(1, COL_BLOCKS) as cb:
                for jt in range(ROW_TILES):
                    unit_step(cb, jt, False)
            store(COL_BLOCKS - 1, ROW_TILES - 1, UNITS - 1)
            for s in range(2):
                sp.wait_ge(stored[s], 16 * UNITS)

        @block.tensor
        def _(pe):
            pe.wait_ge(weights_in, 32)

            def unit_step(unit, primed):
                for q in range(QUARTERS):
                    pe.wait_ge(x_in[q], 16 * (unit + 1))
                    for g in range(QSTEPS):
                        step = unit * STEPS + (q * QSTEPS + g)
                        if primed or q:
                            pe.wait_ge(staged, step - (PSUM_SLOTS - 1))
                        for i in range(GCOLS):
                            last = nc.tensor.matmul(ps[:, g, i, :], x_tile[:, q, g * GCOLS + i, :], w_ab[:, :],
                                                    start=i % 2 == 0, stop=True, skip_group_check=True)
                        last.then_inc(products, 1)

            for jt in range(ROW_TILES):
                unit_step(jt, jt > 0)
            with pe.Fori(1, COL_BLOCKS) as cb:
                for jt in range(ROW_TILES):
                    unit_step(cb * ROW_TILES + jt, True)

        @block.vector
        def _(dve):
            dve.wait_ge(bias_in, 32)

            def unit_step(unit, jt, primed):
                if primed:
                    dve.wait_ge(stored[jt % 2], 16 * (unit - jt % 2))
                for s in range(STEPS):
                    dve.wait_ge(products, unit * STEPS + (s + 1))
                    nc.vector.tensor_tensor(
                        stage[:, jt % 2, :, s * GCOLS:(s + 1) * GCOLS],
                        ps[:, s % PSUM_SLOTS, :, :].rearrange("p i c -> p c i"),
                        bias_ab[:, :].unsqueeze(2).to_broadcast([P, 2 * P, GCOLS]), ALU.add).then_inc(staged, 1)

            for jt in range(ROW_TILES):
                unit_step(jt, jt, jt >= 2)
            with dve.Fori(1, COL_BLOCKS) as cb:
                for jt in range(ROW_TILES):
                    unit_step(cb * ROW_TILES + jt, jt, True)


def contract(nc, ab_scratch, u_scratch):
    with ExitStack() as ctx:
        sb = lambda name, shape, dt=F32: ctx.enter_context(nc.sbuf_tensor(name, shape, dt))
        sem = lambda name: ctx.enter_context(nc.semaphore(name))
        group_ab = sb("group_ab", [P, 2, 2, COL_BLOCKS, ROW_TILES, GROUP, COL_BLOCK], F32R)
        high = sb("ab_high", [P, 2, 2, ROW_TILES, N], F32R)
        b_lows = sb("b_low", [P, 2, ROW_TILES, N], F32R)
        u_out = sb("u_out", [P, 2, ROW_TILES, N])
        ps = ctx.enter_context(nc.psum_tensor("ps_u", [P, 2, ROW_TILES, N], F32))
        loaded = [sem(f"p2_loaded{s}") for s in range(2)]
        highs = sem("p2_highs")
        lows = sem("p2_lows")
        products = sem("p2_products")
        evacuated = sem("p2_evacuated")
        stored = [sem(f"p2_stored{s}") for s in range(2)]
        block = ctx.enter_context(nc.Block())

        def raw(slot, ab, c):
            return group_ab[:, slot, ab, :, :, c, :]

        def by_block(rows):
            return rows.rearrange("p t (b i) -> p b t i", i=COL_BLOCK)

        @block.sync
        def _(sp):
            def load(group, slot):
                for ab in range(2):
                    sp.dma_start(
                        group_ab[:, slot, ab].rearrange("p b t c i -> p (b t) (c i)").bitcast(F32),
                        ab_scratch[group, ab].rearrange("b t p f -> p (b t) f")).then_inc(loaded[slot], 16)

            def store(group, c):
                channel = group * GROUP + c
                sp.wait_ge(evacuated, channel + 1)
                for kt in range(ROW_TILES):
                    sp.dma_start(
                        u_scratch[channel, :, kt * P:(kt + 1) * P, :].rearrange("t k r -> k t r"),
                        u_out[:, c % 2, kt, :].rearrange("p (t r) -> p t r", r=P)).then_inc(stored[c % 2], 16)

            def group_step(group, slot, more):
                for c in range(GROUP):
                    store(group, c)
                if more:
                    sp.wait_ge(products, GROUP * (group + 1))
                    load(group + 2, slot)

            load(0, 0)
            load(1, 1)
            with sp.Fori(0, GROUPS // 2 - 1) as it:
                for slot in range(2):
                    group_step(it * 2 + slot, slot, True)
            for slot in range(2):
                group_step(GROUPS - 2 + slot, slot, False)
            for s in range(2):
                sp.wait_ge(stored[s], 16 * ROW_TILES * P // 2)

        @block.scalar
        def _(act):
            def cut_high(group, slot, c, primed):
                if c == 0:
                    act.wait_ge(loaded[slot], 16 * group + (32 - 16 * slot))
                if primed:
                    act.wait_ge(products, group * GROUP + (c - 1))
                for ab in range(2):
                    nc.scalar.activation(by_block(high[:, c % 2, ab]), raw(slot, ab, c).bitcast(F32),
                                         ACT.Copy).then_inc(highs, 1)

            def evacuate(group, c, primed):
                act.wait_ge(products, group * GROUP + (c + 1))
                if primed:
                    act.wait_ge(stored[c % 2], 16 * ROW_TILES // 2 * (group * GROUP + c - c % 2))
                nc.scalar.activation(u_out[:, c % 2, :, :], ps[:, c % 2, :, :], ACT.Copy).then_inc(evacuated, 1)

            def group_step(group, slot, first, last):
                for c in range(GROUP):
                    evacuate(group, c, not (first and c < 2))
                    if c < 2:
                        cut_high(group, slot, c + 2, True)
                    elif not last:
                        cut_high(group + 1, 1 - slot, c - 2, True)

            cut_high(0, 0, 0, False)
            cut_high(0, 0, 1, False)
            for slot in range(2):
                group_step(slot, slot, slot == 0, False)
            with act.Fori(1, GROUPS // 2 - 1) as it:
                for slot in range(2):
                    group_step(it * 2 + slot, slot, False, False)
            for slot in range(2):
                group_step(GROUPS - 2 + slot, slot, False, slot == 1)

        @block.vector
        def _(dve):
            with dve.Fori(0, GROUPS // 2) as it:
                for slot in range(2):
                    for c in range(GROUP):
                        channel = it * (2 * GROUP) + (slot * GROUP + c)
                        for ab in range(2):
                            dve.wait_ge(highs, channel * 2 + (ab + 1))
                            low = by_block(b_lows[:, c % 2]) if ab else raw(slot, 0, c)
                            nc.vector.tensor_tensor(low, raw(slot, ab, c).bitcast(F32),
                                                    by_block(high[:, c % 2, ab]).bitcast(F32), ALU.subtract).then_inc(lows, 1)

        @block.tensor
        def _(pe):
            def channel_step(group, slot, c, primed):
                channel = group * GROUP + c
                pe.wait_ge(lows, channel * 2 + 2)
                if primed:
                    pe.wait_ge(evacuated, channel - 1)
                for kt in range(ROW_TILES):
                    columns = slice(kt * P, (kt + 1) * P)
                    for jt in range(ROW_TILES):
                        a_high = high[:, c % 2, 0, jt, :]
                        a_low = group_ab[:, slot, 0, :, jt, c, :]
                        b_high = high[:, c % 2, 1, jt, columns]
                        b_low = b_lows[:, c % 2, jt, columns]
                        acc = ps[:, c % 2, kt, :]
                        nc.tensor.matmul(acc, b_high, a_high, start=jt == 0, stop=False)
                        nc.tensor.matmul(acc, b_high, a_low, start=False, stop=False)
                        last = nc.tensor.matmul(acc, b_low, a_high, start=False, stop=jt == ROW_TILES - 1)
                last.then_inc(products, 1)

            for slot in range(2):
                for c in range(GROUP):
                    channel_step(slot, slot, c, slot > 0 or c >= 2)
            with pe.Fori(1, GROUPS // 2) as it:
                for slot in range(2):
                    for c in range(GROUP):
                        channel_step(it * 2 + slot, slot, c, True)


def finish(nc, xT, Wg, Wo, bg, bo, gamma, beta, u_scratch, out):
    RING = 3
    SUBS = CHUNK // N
    TILES = N // P
    PAIRS = CHUNKS * SUBS // 2
    BODY = RING * SUBS // 2
    LOOPS = PAIRS // BODY
    PT = 2 * TILES
    with ExitStack() as ctx:
        sb = lambda name, shape, dt=F32: ctx.enter_context(nc.sbuf_tensor(name, shape, dt))
        sem = lambda name: ctx.enter_context(nc.semaphore(name))
        w_g = sb("w_g", [P, P])
        w_o = sb("w_o", [P, P])
        ident = sb("ident", [P, P])
        bias_g = sb("bias_g", [P, 1])
        gamma_b = sb("gamma_b", [P, P])
        beta_b = sb("beta_b", [P, P])
        bo_rest = sb("bo_rest", [3, N])
        bo_part = sb("bo_part", [3, 3, N], BF16)
        bo_split = sb("bo_split", [3, N], BF16)
        bo_sum = sb("bo_sum", [3, N])
        ones3 = sb("ones3", [3, P], BF16)
        x_t = sb("x_t", [P, RING, SUBS, N])
        u_t = sb("u_t", [P, RING, SUBS, N])
        o_t = sb("o_t", [P, RING, CHUNK_COLS, P])
        gate = sb("gate", [P, 2, N])
        gated = sb("gated", [P, 4, N])
        stats = sb("stats", [P, 2, PT, 6])
        sums = sb("sums", [P, 2, PT, 2])
        diff = sb("diff", [P, 2, PT])
        sqdiff = sb("sqdiff", [P, 2, PT])
        var = sb("var", [P, 2, PT])
        minus_half = sb("minus_half", [P, PT])
        scale = sb("scale", [P, 2, PT])
        minus_mean = sb("minus_mean", [P, 2, PT])
        shift = sb("shift", [P, 2, PT])
        ps_g = ctx.enter_context(nc.psum_tensor("ps_g", [P, 2, N], F32))
        ps_o = ctx.enter_context(nc.psum_tensor("ps_o", [P, 3, 2, TILES, P], F32))
        consts_in = sem("p3_consts_in")
        setup = sem("p3_setup")
        bo_chain = sem("p3_bo_chain")
        consts_ready = sem("p3_consts_ready")
        x_in = [sem(f"p3_x_in{s}") for s in range(RING)]
        u_in = [sem(f"p3_u_in{s}") for s in range(RING)]
        gate_sums = sem("p3_gate_sums")
        gates = sem("p3_gates")
        gateds = sem("p3_gateds")
        outputs = sem("p3_outputs")
        stats_done = sem("p3_stats_done")
        chain = sem("p3_chain")
        norms_ready = sem("p3_norms_ready")
        normed = sem("p3_normed")
        scaled = sem("p3_scaled")
        finished = sem("p3_finished")
        stored = [sem(f"p3_stored{s}") for s in range(RING)]
        block = ctx.enter_context(nc.Block())

        def at_least(index, bound):
            return not isinstance(index, int) or index >= bound

        def below(index, bound):
            return not isinstance(index, int) or index < bound

        def run_pairs(engine, step):
            for k in range(BODY):
                step(k, k)
            with engine.Fori(1, LOOPS) as it:
                for k in range(BODY):
                    step(it * BODY + k, k)
            for k in range(PAIRS - LOOPS * BODY):
                step(LOOPS * BODY + k, k)

        def o_half(k, h):
            k = k % BODY
            first = (k % 2) * PT + h * TILES
            return o_t[:, k // 2, first:first + TILES, :]

        def o_pair(k):
            k = k % BODY
            return o_t[:, k // 2, (k % 2) * PT:(k % 2 + 1) * PT, :]

        @block.sync
        def _(sp):
            sp.dma_start(w_g[:, :], Wg).then_inc(consts_in, 16)
            sp.dma_start(w_o[:, :], Wo).then_inc(consts_in, 16)
            sp.dma_start(bias_g[:, :], bg[:, None]).then_inc(consts_in, 16)
            sp.dma_start(gamma_b[:, :], gamma[None, :].to_broadcast([P, P])).then_inc(consts_in, 16)
            sp.dma_start(beta_b[:, :], beta[None, :].to_broadcast([P, P])).then_inc(consts_in, 16)
            for t in range(TILES):
                sp.dma_start(bo_rest[:, t * P:(t + 1) * P], bo[None, :].to_broadcast([3, P])).then_inc(consts_in, 16)

            def load(chunk, slot):
                sp.dma_start(x_t[:, slot].rearrange("p a b -> p (a b)"), xT[chunk]).then_inc(x_in[slot], 16)
                sp.dma_start(u_t[:, slot].rearrange("p a b -> p (a b)"),
                             u_scratch[:, chunk, :]).then_inc(u_in[slot], 16)

            def chunk_step(chunk, slot, more):
                if more:
                    sp.wait_ge(outputs, SUBS * (chunk + 1))
                    load(chunk + RING, slot)
                sp.wait_ge(finished, 2 * (chunk + 1))
                sp.dma_start(out[chunk], o_t[:, slot].rearrange("p a b -> p (a b)")).then_inc(stored[slot], 16)

            for chunk in range(RING):
                load(chunk, chunk)
            with sp.Fori(0, CHUNKS // RING - 1) as it:
                for slot in range(RING):
                    chunk_step(it * RING + slot, slot, True)
            for chunk in range((CHUNKS // RING - 1) * RING, CHUNKS):
                chunk_step(chunk, chunk % RING, chunk + RING < CHUNKS)
            for slot in range(RING):
                sp.wait_ge(stored[slot], 16 * len(range(slot, CHUNKS, RING)))

        @block.tensor
        def _(pe):
            pe.wait_ge(consts_in, 16 * (5 + TILES))
            pe.wait_ge(consts_ready, 2)

            def gate_product(pair, k, h):
                step = pair * 2 + h
                slot = (k % BODY) // 2
                if k % 2 == 0 and h == 0:
                    pe.wait_ge(x_in[slot], x_count(pair, k))
                if at_least(pair, 1):
                    pe.wait_ge(gates, step - 1)
                nc.tensor.matmul(ps_g[:, h, :], w_g[:, :], x_t[:, slot, 2 * (k % 2) + h, :],
                                 start=True, stop=True).then_inc(gate_sums, 1)

            def x_count(pair, k):
                if isinstance(pair, int):
                    return 16 * (pair // BODY + 1)
                return (pair - k % BODY + (BODY if k >= BODY else 0) - (BODY if k >= BODY else 0)) * 16 // BODY + 16

            def output(pair, k, h):
                step = pair * 2 + h
                slot = k // 2
                sub = 2 * (k % 2) + h
                if at_least(pair, 3) and h == 0:
                    pe.wait_ge(normed, 2 * pair - 4)
                pe.wait_ge(gateds, step + 1)
                nc.tensor.matmul(ps_o[:, k % 3, h].rearrange("p t c -> p (t c)"), ones3[:, :], bo_split[:, :],
                                 start=True, stop=False, skip_group_check=True)
                for t in range(TILES):
                    acc = ps_o[:, k % 3, h, t, :]
                    nc.tensor.matmul(acc, x_t[:, slot, sub, t * P:(t + 1) * P], ident[:, :], is_transpose=True,
                                     start=False, stop=False, skip_group_check=True)
                    last = nc.tensor.matmul(acc, gated[:, sub, t * P:(t + 1) * P], w_o[:, :],
                                            start=False, stop=True, skip_group_check=True)
                last.then_inc(outputs, 1)

            def step(pair, k):
                for h in range(2):
                    output(pair, k, h)
                    if below(pair, PAIRS - 1):
                        gate_product(pair + 1, k + 1, h)

            gate_product(0, 0, 0)
            gate_product(0, 0, 1)
            run_pairs(pe, step)

        @block.scalar
        def _(act):
            act.wait_ge(consts_in, 16 * (5 + TILES))

            def sigmoid(pair, h):
                step = pair * 2 + h
                act.wait_ge(gate_sums, step + 1)
                if at_least(pair, 1):
                    act.wait_ge(gateds, step - 1)
                nc.scalar.activation(gate[:, h, :], ps_g[:, h, :], ACT.Sigmoid,
                                     bias=bias_g[:, 0:1]).then_inc(gates, 1)

            def normalise(pair, k, h):
                if h == 0:
                    act.wait_ge(norms_ready, pair + 1)
                    if k % 2 == 0 and at_least(pair, BODY):
                        act.wait_ge(stored[(k % BODY) // 2], stored_count(pair))
                for t in range(TILES):
                    i = h * TILES + t
                    last = nc.scalar.activation(o_half(k, h)[:, t, :], ps_o[:, k % 3, h, t, :], ACT.Identity,
                                                scale=scale[:, k % 2, i:i + 1], bias=shift[:, k % 2, i:i + 1])
                last.then_inc(normed, 1)

            def stored_count(pair):
                return 16 * (pair // BODY)

            def step(pair, k):
                for h in range(2):
                    if below(pair, PAIRS - 1):
                        sigmoid(pair + 1, h)
                    if at_least(pair, 1):
                        normalise(pair - 1, (k - 1) % BODY, h)

            sigmoid(0, 0)
            sigmoid(0, 1)
            run_pairs(act, step)
            for h in range(2):
                normalise(PAIRS - 1, (PAIRS - 1) % BODY, h)

        @block.vector
        def _(dve):
            dve.wait_ge(consts_in, 16 * (5 + TILES))
            dve.wait_ge(consts_ready, 1)
            for i in range(3):
                nc.vector.tensor_copy(bo_part[:, i, :], bo_rest[:, :]).then_inc(bo_chain, 1)
                dve.wait_ge(bo_chain, 3 * i + 1)
                nc.vector.tensor_tensor(bo_rest[:, :], bo_rest[:, :], bo_part[:, i, :],
                                        ALU.subtract).then_inc(bo_chain, 1)
                if i == 0:
                    nc.vector.tensor_scalar(bo_sum[:, :], bo_part[:, 0, :], ident[0:3, 0:1], None,
                                            ALU.mult).then_inc(bo_chain, 1)
                else:
                    nc.vector.scalar_tensor_tensor(bo_sum[:, :], bo_part[:, i, :], ident[0:3, i:i + 1], bo_sum[:, :],
                                                   ALU.mult, ALU.add).then_inc(bo_chain, 1)
                dve.wait_ge(bo_chain, 3 * i + 3)
            nc.vector.tensor_copy(bo_split[:, :], bo_sum[:, :]).then_inc(consts_ready, 1)

            def gating(pair, k, h):
                step = pair * 2 + h
                slot = (k % BODY) // 2
                sub = 2 * (k % 2) + h
                if k % 2 == 0 and h == 0:
                    dve.wait_ge(u_in[slot], u_count(pair))
                dve.wait_ge(gates, step + 1)
                if at_least(pair, 2):
                    dve.wait_ge(outputs, step - 3)
                nc.vector.tensor_tensor(gated[:, sub, :], gate[:, h, :], u_t[:, slot, sub, :],
                                        ALU.mult).then_inc(gateds, 1)

            def u_count(pair):
                return 16 * (pair // BODY) + 16

            def statistics(pair, k, h):
                dve.wait_ge(outputs, pair * 2 + (h + 1))
                if at_least(pair, 2) and h == 0:
                    dve.wait_ge(norms_ready, pair - 1)
                for t in range(TILES):
                    last = nc.vector.bn_stats(stats[:, k % 2, h * TILES + t, :], ps_o[:, k % 3, h, t, :])
                if h == 1:
                    last.then_inc(stats_done, 1)

            def add_beta(pair, k):
                dve.wait_ge(scaled, pair + 1)
                nc.vector.tensor_tensor(o_pair(k), o_pair(k),
                                        beta_b[:, :].unsqueeze(1).to_broadcast([P, PT, P]),
                                        ALU.add).then_inc(finished, 1)

            def step(pair, k):
                for h in range(2):
                    statistics(pair, k, h)
                    if below(pair, PAIRS - 1):
                        gating(pair + 1, k + 1, h)
                if at_least(pair, 2):
                    add_beta(pair - 2, (k - 2) % BODY)

            gating(0, 0, 0)
            gating(0, 0, 1)
            run_pairs(dve, step)
            for pair in (PAIRS - 2, PAIRS - 1):
                add_beta(pair, pair % BODY)

        @block.gpsimd
        def _(pool):
            nc.gpsimd.memset(ident[:, :], 0.0).then_inc(setup, 1)
            nc.gpsimd.memset(ones3[:, :], 1.0).then_inc(setup, 1)
            nc.gpsimd.memset(minus_half[:, :], -0.5).then_inc(setup, 1)
            pool.wait_ge(setup, 3)
            nc.gpsimd.affine_select(out=ident[:, :], in_=ident[:, :], compare_op=ALU.not_equal, fill=1.0, base=0,
                                    pattern=[[-1, P]], channel_multiplier=1).then_inc(consts_ready, 1)
            pool.wait_ge(consts_in, 16 * (5 + TILES))
            nc.gpsimd.tensor_scalar(gamma_b[:, :], gamma_b[:, :], 2.0, None, ALU.mult).then_inc(setup, 1)
            pool.wait_ge(setup, 4)

            def small_steps(pair, k):
                s = k % 2
                pool.wait_ge(stats_done, pair + 1)
                if at_least(pair, 2):
                    pool.wait_ge(normed, 2 * pair - 2)
                nc.gpsimd.tensor_tensor(diff[:, s], stats[:, s, :, 1], stats[:, s, :, 4],
                                        ALU.subtract).then_inc(chain, 1)
                nc.gpsimd.tensor_tensor(sums[:, s], stats[:, s, :, 1:3], stats[:, s, :, 4:6],
                                        ALU.add).then_inc(chain, 1)
                pool.wait_ge(chain, pair * 7 + 2)
                nc.gpsimd.tensor_tensor(sqdiff[:, s], diff[:, s], diff[:, s], ALU.mult).then_inc(chain, 1)
                nc.gpsimd.tensor_scalar(var[:, s], sums[:, s, :, 1], 4.0 / P, 4 * EPS,
                                        ALU.mult, ALU.add).then_inc(chain, 1)
                nc.gpsimd.tensor_scalar(minus_mean[:, s], sums[:, s, :, 0], -0.5, None, ALU.mult).then_inc(chain, 1)
                pool.wait_ge(chain, pair * 7 + 4)
                nc.gpsimd.tensor_tensor(var[:, s], var[:, s], sqdiff[:, s], ALU.add).then_inc(chain, 1)
                pool.wait_ge(chain, pair * 7 + 6)
                nc.gpsimd.tensor_tensor(scale[:, s], var[:, s], minus_half[:, :], ALU.pow).then_inc(chain, 1)
                pool.wait_ge(chain, pair * 7 + 7)
                nc.gpsimd.tensor_tensor(shift[:, s], minus_mean[:, s], scale[:, s],
                                        ALU.mult).then_inc(norms_ready, 1)

            def times_gamma(pair, k):
                pool.wait_ge(normed, pair * 2 + 2)
                nc.gpsimd.tensor_tensor(o_pair(k), o_pair(k),
                                        gamma_b[:, :].unsqueeze(1).to_broadcast([P, PT, P]),
                                        ALU.mult).then_inc(scaled, 1)

            def step(pair, k):
                small_steps(pair, k)
                if at_least(pair, 1):
                    times_gamma(pair - 1, (k - 1) % BODY)

            run_pairs(pool, step)
            times_gamma(PAIRS - 1, (PAIRS - 1) % BODY)


def build(nc, xT, Wa, ba, Wb, bb, Wg, bg, Wo, bo, gamma, beta, out):
    ab_scratch = nc.dram_tensor("ab_scratch", [GROUPS, 2, COL_BLOCKS, ROW_TILES, P, RUN], F32, kind="Internal").ap()
    u_store = nc.dram_tensor("u_scratch", [P, N * N + PAD], F32, kind="Internal").ap()
    u_values = u_store[:, 0:N * N]
    project(nc, xT, Wa, Wb, ba, bb, ab_scratch)
    contract(nc, ab_scratch, u_values.rearrange("c (t k r) -> c t k r", t=ROW_TILES, k=N))
    finish(nc, xT, Wg, Wo, bg, bo, gamma, beta, u_values.rearrange("c (m f) -> c m f", m=CHUNKS), out)


_NAMES = ["L0_conv_Wa", "L0_conv_ba", "L0_conv_Wb", "L0_conv_bb", "L0_conv_Wg", "L0_conv_bg",
          "L0_conv_Wo", "L0_conv_bo", "L0_conv_gamma", "L0_conv_beta"]


def kernel(**inputs):
    import concourse.bacc as bacc
    from concourse.bass_utils import run_bass_kernel_spmd

    nc = bacc.Bacc("TRN2", target_bir_lowering=False, num_devices=1)
    x = np.asarray(inputs["x"])[0]
    blocks = N // CHUNK_COLS
    x = x.reshape(ROW_TILES, P, blocks, CHUNK_COLS, P).transpose(0, 2, 4, 3, 1)
    arrays = {"in_xT": np.ascontiguousarray(x).reshape(CHUNKS, P, CHUNK)}
    for name in _NAMES:
        arrays["in_" + name] = np.ascontiguousarray(inputs[name])
    args = [nc.dram_tensor(n, a.shape, mybir.dt.from_np(a.dtype), kind="ExternalInput").ap()
            for n, a in arrays.items()]
    out = nc.dram_tensor("out_dram", (CHUNKS, P, CHUNK), F32, kind="ExternalOutput").ap()
    build(nc, *args, out)
    r = run_bass_kernel_spmd(nc, [arrays], core_ids=[0])
    got = np.asarray(r.results[0]["out_dram"]).reshape(ROW_TILES, blocks, P, CHUNK_COLS, P)
    return np.ascontiguousarray(got.transpose(0, 2, 1, 3, 4)).reshape(1, N, N, P)
```

```python
from contextlib import ExitStack

import numpy as np
import concourse.bass as bass
from concourse import mybir
from concourse.alu_op_type import AluOpType as ALU

F32 = mybir.dt.float32
F32R = mybir.dt.float32r
I32 = mybir.dt.int32
BF16 = mybir.dt.bfloat16
ACT = mybir.ActivationFunctionType

P = 128
N = 512
ROW_TILES = N // P
COL_BLOCK = 64
COL_BLOCKS = N // COL_BLOCK
UNITS = COL_BLOCKS * ROW_TILES
CHUNK_COLS = 16
QUARTERS = COL_BLOCK // CHUNK_COLS
CHUNK = CHUNK_COLS * P
CHUNKS = N * N // CHUNK
GROUP = 4
GROUPS = P // GROUP
RUN = GROUP * COL_BLOCK
PAD = 1024
EPS = 1e-5


def project(nc, xT, Wa, Wb, ba, bb, ab_scratch):
    PSUM_SLOTS = 4
    GCOLS = 4
    STEPS = COL_BLOCK // GCOLS
    QSTEPS = STEPS // QUARTERS
    with ExitStack() as ctx:
        sb = lambda name, shape, dt=F32: ctx.enter_context(nc.sbuf_tensor(name, shape, dt))
        sem = lambda name: ctx.enter_context(nc.semaphore(name))
        w_ab = sb("w_ab", [P, 2 * P])
        bias_ab = sb("bias_ab", [P, 2 * P])
        x_tile = sb("x_tile", [P, QUARTERS, CHUNK_COLS, P])
        stage = sb("stage", [P, 2, 2 * P, COL_BLOCK])
        ps = ctx.enter_context(nc.psum_tensor("ps_ab", [P, PSUM_SLOTS, GCOLS, 2 * P], F32))
        weights_in = sem("p1_weights_in")
        bias_in = sem("p1_bias_in")
        x_in = [sem(f"p1_x_in{q}") for q in range(QUARTERS)]
        products = sem("p1_products")
        staged = sem("p1_staged")
        stored = [sem(f"p1_stored{s}") for s in range(2)]
        block = ctx.enter_context(nc.Block())

        @block.sync
        def _(sp):
            sp.dma_start(w_ab[:, 0:P], Wa).then_inc(weights_in, 16)
            sp.dma_start(w_ab[:, P:2 * P], Wb).then_inc(weights_in, 16)
            sp.dma_start(bias_ab[:, 0:P], ba[None, :].to_broadcast([P, P])).then_inc(bias_in, 16)
            sp.dma_start(bias_ab[:, P:2 * P], bb[None, :].to_broadcast([P, P])).then_inc(bias_in, 16)

            def store(cb, jt, unit):
                sp.wait_ge(staged, STEPS * (unit + 1))
                for ab in range(2):
                    sp.dma_start(
                        ab_scratch[:, ab, cb, jt, :, :].rearrange("g p f -> p g f"),
                        stage[:, jt % 2, ab * P:(ab + 1) * P, :].rearrange("p (g c) i -> p g (c i)", c=GROUP),
                    ).then_inc(stored[jt % 2], 16)

            def unit_step(cb, jt, first):
                unit = cb * ROW_TILES + jt
                for q in range(QUARTERS):
                    if not first:
                        sp.wait_ge(products, STEPS * (unit - 1) + QSTEPS * (q + 1))
                    sp.dma_start(x_tile[:, q, :, :].rearrange("p a b -> p (a b)"),
                                 xT[cb * QUARTERS + (jt * (N // CHUNK_COLS) + q), :, :]).then_inc(x_in[q], 16)
                if not first:
                    if jt:
                        store(cb, jt - 1, unit - 1)
                    else:
                        store(cb - 1, ROW_TILES - 1, unit - 1)

            for jt in range(ROW_TILES):
                unit_step(0, jt, jt == 0)
            with sp.Fori(1, COL_BLOCKS) as cb:
                for jt in range(ROW_TILES):
                    unit_step(cb, jt, False)
            store(COL_BLOCKS - 1, ROW_TILES - 1, UNITS - 1)
            for s in range(2):
                sp.wait_ge(stored[s], 16 * UNITS)

        @block.tensor
        def _(pe):
            pe.wait_ge(weights_in, 32)

            def unit_step(unit, primed):
                for q in range(QUARTERS):
                    pe.wait_ge(x_in[q], 16 * (unit + 1))
                    for g in range(QSTEPS):
                        step = unit * STEPS + (q * QSTEPS + g)
                        if primed or q:
                            pe.wait_ge(staged, step - (PSUM_SLOTS - 1))
                        for i in range(GCOLS):
                            last = nc.tensor.matmul(ps[:, g, i, :], x_tile[:, q, g * GCOLS + i, :], w_ab[:, :],
                                                    start=i % 2 == 0, stop=True, skip_group_check=True)
                        last.then_inc(products, 1)

            for jt in range(ROW_TILES):
                unit_step(jt, jt > 0)
            with pe.Fori(1, COL_BLOCKS) as cb:
                for jt in range(ROW_TILES):
                    unit_step(cb * ROW_TILES + jt, True)

        @block.vector
        def _(dve):
            dve.wait_ge(bias_in, 32)

            def unit_step(unit, jt, primed):
                if primed:
                    dve.wait_ge(stored[jt % 2], 16 * (unit - jt % 2))
                for s in range(STEPS):
                    dve.wait_ge(products, unit * STEPS + (s + 1))
                    nc.vector.tensor_tensor(
                        stage[:, jt % 2, :, s * GCOLS:(s + 1) * GCOLS],
                        ps[:, s % PSUM_SLOTS, :, :].rearrange("p i c -> p c i"),
                        bias_ab[:, :].unsqueeze(2).to_broadcast([P, 2 * P, GCOLS]), ALU.add).then_inc(staged, 1)

            for jt in range(ROW_TILES):
                unit_step(jt, jt, jt >= 2)
            with dve.Fori(1, COL_BLOCKS) as cb:
                for jt in range(ROW_TILES):
                    unit_step(cb * ROW_TILES + jt, jt, True)


def contract(nc, ab_scratch, u_scratch):
    with ExitStack() as ctx:
        sb = lambda name, shape, dt=F32: ctx.enter_context(nc.sbuf_tensor(name, shape, dt))
        sem = lambda name: ctx.enter_context(nc.semaphore(name))
        group_ab = sb("group_ab", [P, 2, 2, COL_BLOCKS, ROW_TILES, GROUP, COL_BLOCK], F32R)
        high = sb("ab_high", [P, 2, 2, ROW_TILES, N], F32R)
        b_lows = sb("b_low", [P, 2, ROW_TILES, N], F32R)
        u_out = sb("u_out", [P, 2, ROW_TILES, N])
        ps = ctx.enter_context(nc.psum_tensor("ps_u", [P, 2, ROW_TILES, N], F32))
        loaded = [sem(f"p2_loaded{s}") for s in range(2)]
        highs = sem("p2_highs")
        lows = sem("p2_lows")
        products = sem("p2_products")
        evacuated = sem("p2_evacuated")
        stored = [sem(f"p2_stored{s}") for s in range(2)]
        block = ctx.enter_context(nc.Block())

        def raw(slot, ab, c):
            return group_ab[:, slot, ab, :, :, c, :]

        def by_block(rows):
            return rows.rearrange("p t (b i) -> p b t i", i=COL_BLOCK)

        @block.sync
        def _(sp):
            def load(group, slot):
                for ab in range(2):
                    sp.dma_start(
                        group_ab[:, slot, ab].rearrange("p b t c i -> p (b t) (c i)").bitcast(F32),
                        ab_scratch[group, ab].rearrange("b t p f -> p (b t) f")).then_inc(loaded[slot], 16)

            def store(group, c):
                channel = group * GROUP + c
                sp.wait_ge(evacuated, channel + 1)
                for kt in range(ROW_TILES):
                    sp.dma_start(
                        u_scratch[channel, :, kt * P:(kt + 1) * P, :].rearrange("t k r -> k t r"),
                        u_out[:, c % 2, kt, :].rearrange("p (t r) -> p t r", r=P)).then_inc(stored[c % 2], 16)

            def group_step(group, slot, more):
                for c in range(GROUP):
                    store(group, c)
                if more:
                    sp.wait_ge(products, GROUP * (group + 1))
                    load(group + 2, slot)

            load(0, 0)
            load(1, 1)
            with sp.Fori(0, GROUPS // 2 - 1) as it:
                for slot in range(2):
                    group_step(it * 2 + slot, slot, True)
            for slot in range(2):
                group_step(GROUPS - 2 + slot, slot, False)
            for s in range(2):
                sp.wait_ge(stored[s], 16 * ROW_TILES * P // 2)

        @block.scalar
        def _(act):
            def cut_high(group, slot, c, primed):
                if c == 0:
                    act.wait_ge(loaded[slot], 16 * group + (32 - 16 * slot))
                if primed:
                    act.wait_ge(products, group * GROUP + (c - 1))
                for ab in range(2):
                    nc.scalar.activation(by_block(high[:, c % 2, ab]), raw(slot, ab, c).bitcast(F32),
                                         ACT.Copy).then_inc(highs, 1)

            def evacuate(group, c, primed):
                act.wait_ge(products, group * GROUP + (c + 1))
                if primed:
                    act.wait_ge(stored[c % 2], 16 * ROW_TILES // 2 * (group * GROUP + c - c % 2))
                nc.scalar.activation(u_out[:, c % 2, :, :], ps[:, c % 2, :, :], ACT.Copy).then_inc(evacuated, 1)

            def group_step(group, slot, first, last):
                for c in range(GROUP):
                    evacuate(group, c, not (first and c < 2))
                    if c < 2:
                        cut_high(group, slot, c + 2, True)
                    elif not last:
                        cut_high(group + 1, 1 - slot, c - 2, True)

            cut_high(0, 0, 0, False)
            cut_high(0, 0, 1, False)
            for slot in range(2):
                group_step(slot, slot, slot == 0, False)
            with act.Fori(1, GROUPS // 2 - 1) as it:
                for slot in range(2):
                    group_step(it * 2 + slot, slot, False, False)
            for slot in range(2):
                group_step(GROUPS - 2 + slot, slot, False, slot == 1)

        @block.vector
        def _(dve):
            with dve.Fori(0, GROUPS // 2) as it:
                for slot in range(2):
                    for c in range(GROUP):
                        channel = it * (2 * GROUP) + (slot * GROUP + c)
                        for ab in range(2):
                            dve.wait_ge(highs, channel * 2 + (ab + 1))
                            low = by_block(b_lows[:, c % 2]) if ab else raw(slot, 0, c)
                            nc.vector.tensor_tensor(low, raw(slot, ab, c).bitcast(F32),
                                                    by_block(high[:, c % 2, ab]).bitcast(F32), ALU.subtract).then_inc(lows, 1)

        @block.tensor
        def _(pe):
            def channel_step(group, slot, c, primed):
                channel = group * GROUP + c
                pe.wait_ge(lows, channel * 2 + 2)
                if primed:
                    pe.wait_ge(evacuated, channel - 1)
                for kt in range(ROW_TILES):
                    columns = slice(kt * P, (kt + 1) * P)
                    for jt in range(ROW_TILES):
                        a_high = high[:, c % 2, 0, jt, :]
                        a_low = group_ab[:, slot, 0, :, jt, c, :]
                        b_high = high[:, c % 2, 1, jt, columns]
                        b_low = b_lows[:, c % 2, jt, columns]
                        acc = ps[:, c % 2, kt, :]
                        nc.tensor.matmul(acc, b_high, a_high, start=jt == 0, stop=False)
                        nc.tensor.matmul(acc, b_high, a_low, start=False, stop=False)
                        last = nc.tensor.matmul(acc, b_low, a_high, start=False, stop=jt == ROW_TILES - 1)
                last.then_inc(products, 1)

            for slot in range(2):
                for c in range(GROUP):
                    channel_step(slot, slot, c, slot > 0 or c >= 2)
            with pe.Fori(1, GROUPS // 2) as it:
                for slot in range(2):
                    for c in range(GROUP):
                        channel_step(it * 2 + slot, slot, c, True)


def finish(nc, xT, Wg, Wo, bg, bo, gamma, beta, u_scratch, out):
    RING = 3
    TILES = 4
    SUBS = CHUNK_COLS // TILES
    STEPS = CHUNKS * SUBS
    BODY = RING * SUBS
    LOOPS = STEPS // BODY
    BANKS = 6
    AHEAD = 2
    BETA_SPLIT = 3
    BATCH = 3
    BATCH_TILES = BATCH * TILES
    BATCHES = BODY // BATCH
    ROOT_ROUNDS = 3
    ROOT_SEED = float(0x5F3759DF)
    CHAIN = 8 + 3 * ROOT_ROUNDS - 1
    NORM_LAG, GAMMA_LAG, BETA_LAG = 5, 6, 7
    with ExitStack() as ctx:
        sb = lambda name, shape, dt=F32: ctx.enter_context(nc.sbuf_tensor(name, shape, dt))
        sem = lambda name: ctx.enter_context(nc.semaphore(name))
        w_g = sb("w_g", [P, P])
        w_o = sb("w_o", [P, P])
        ident = sb("ident", [P, P])
        bias_g = sb("bias_g", [P, 1])
        gamma_b = sb("gamma_b", [P, P])
        beta_b = sb("beta_b", [P, P])
        bo_rest = sb("bo_rest", [3, N])
        bo_part = sb("bo_part", [3, 3, N], BF16)
        bo_split = sb("bo_split", [3, N], BF16)
        bo_sum = sb("bo_sum", [3, N])
        ones3 = sb("ones3", [3, P], BF16)
        x_t = sb("x_t", [P, RING, SUBS, N])
        u_t = sb("u_t", [P, RING, SUBS, N])
        o_t = sb("o_t", [P, RING, CHUNK_COLS, P])
        gated = sb("gated", [P, SUBS, N])
        stats = sb("stats", [P, BATCHES, BATCH_TILES, 6])
        sums = sb("sums", [P, BATCHES, BATCH_TILES, 2])
        diff = sb("diff", [P, BATCHES, BATCH_TILES])
        sqdiff = sb("sqdiff", [P, BATCHES, BATCH_TILES])
        var_part = sb("var_part", [P, BATCHES, BATCH_TILES])
        var = sb("var", [P, BATCHES, BATCH_TILES])
        scale = sb("scale", [P, BATCHES, ROOT_ROUNDS + 1, BATCH_TILES])
        root = sb("root", [P, BATCHES, ROOT_ROUNDS, BATCH_TILES])
        residual = sb("residual", [P, BATCHES, ROOT_ROUNDS, BATCH_TILES])
        shift = sb("shift", [P, BATCHES, BATCH_TILES])
        ps_g = ctx.enter_context(nc.psum_tensor("ps_g", [P, 2, N], F32))
        ps_o = ctx.enter_context(nc.psum_tensor("ps_o", [P, BANKS, TILES, P], F32))
        consts_in = sem("p3_consts_in")
        setup = sem("p3_setup")
        bo_chain = sem("p3_bo_chain")
        consts_ready = sem("p3_consts_ready")
        x_in = [sem(f"p3_x_in{s}") for s in range(RING)]
        u_in = [sem(f"p3_u_in{s}") for s in range(RING)]
        gate_sums = sem("p3_gate_sums")
        gates = sem("p3_gates")
        gateds = sem("p3_gateds")
        outputs = sem("p3_outputs")
        chain = sem("p3_chain")
        shifts = sem("p3_shifts")
        normed = sem("p3_normed")
        scaled = sem("p3_scaled")
        finished_pool = sem("p3_finished_pool")
        finished_dve = sem("p3_finished_dve")
        stored = [sem(f"p3_stored{s}") for s in range(RING)]
        block = ctx.enter_context(nc.Block())


        def moved(lap, k, by):
            return lap + (k + by) // BODY, (k + by) % BODY

        def at_least(lap, k, bound):
            return not isinstance(lap, int) or lap * BODY + k >= bound

        def exists(lap, k, ahead):
            return not isinstance(lap, int) or lap * BODY + k + ahead < STEPS

        def run_steps(engine, body):
            for k in range(BODY):
                body(0, k)
            with engine.Fori(1, LOOPS) as lap:
                for k in range(BODY):
                    body(lap, k)
            for k in range(STEPS - LOOPS * BODY):
                body(LOOPS, k)

        def o_step(k):
            return o_t[:, k // SUBS, k % SUBS * TILES:(k % SUBS + 1) * TILES, :]

        @block.sync
        def _(sp):
            sp.dma_start(w_g[:, :], Wg).then_inc(consts_in, 16)
            sp.dma_start(w_o[:, :], Wo).then_inc(consts_in, 16)
            sp.dma_start(bias_g[:, :], bg[:, None]).then_inc(consts_in, 16)
            sp.dma_start(gamma_b[:, :], gamma[None, :].to_broadcast([P, P])).then_inc(consts_in, 16)
            sp.dma_start(beta_b[:, :], beta[None, :].to_broadcast([P, P])).then_inc(consts_in, 16)
            for t in range(TILES):
                sp.dma_start(bo_rest[:, t * P:(t + 1) * P], bo[None, :].to_broadcast([3, P])).then_inc(consts_in, 16)

            def load(chunk, slot):
                sp.dma_start(x_t[:, slot].rearrange("p a b -> p (a b)"), xT[chunk]).then_inc(x_in[slot], 16)
                sp.dma_start(u_t[:, slot].rearrange("p a b -> p (a b)"),
                             u_scratch[:, chunk, :]).then_inc(u_in[slot], 16)

            def store(chunk, slot):
                sp.wait_ge(finished_pool, SUBS * (chunk + 1))
                sp.wait_ge(finished_dve, SUBS * (chunk + 1))
                sp.dma_start(out[chunk], o_t[:, slot].rearrange("p a b -> p (a b)")).then_inc(stored[slot], 16)

            def reload(chunk, slot):
                sp.wait_ge(outputs, SUBS * (chunk + 1))
                load(chunk + RING, slot)

            for chunk in range(RING):
                load(chunk, chunk)
            reload(0, 0)
            reload(1, 1)
            with sp.Fori(0, (CHUNKS - 5) // RING) as lap:
                for slot in range(RING):
                    store(lap * RING + slot, slot)
                    reload(lap * RING + (slot + 2), (slot + 2) % RING)
            for chunk in range(CHUNKS - 5, CHUNKS):
                store(chunk, chunk % RING)
            for slot in range(RING):
                sp.wait_ge(stored[slot], 16 * len(range(slot, CHUNKS, RING)))

        @block.tensor
        def _(pe):
            pe.wait_ge(consts_in, 16 * (5 + TILES))
            pe.wait_ge(consts_ready, 2)

            def gate_product(lap, k):
                step = lap * BODY + k
                if k % SUBS == 0:
                    pe.wait_ge(x_in[k // SUBS], lap * 16 + 16)
                if at_least(lap, k, 2):
                    pe.wait_ge(gateds, step - 1)
                nc.tensor.matmul(ps_g[:, k % 2, :], w_g[:, :], x_t[:, k // SUBS, k % SUBS, :],
                                 start=True, stop=True).then_inc(gate_sums, 1)

            def output(lap, k):
                step = lap * BODY + k
                bank = k % BANKS
                if at_least(lap, k, BANKS):
                    pe.wait_ge(normed, step - (BANKS - 1))
                pe.wait_ge(gateds, step + 1)
                nc.tensor.matmul(ps_o[:, bank].rearrange("p t c -> p (t c)"), ones3[:, :], bo_split[:, :],
                                 start=True, stop=False, skip_group_check=True)
                for t in range(TILES):
                    acc = ps_o[:, bank, t, :]
                    rows = slice(t * P, (t + 1) * P)
                    nc.tensor.matmul(acc, x_t[:, k // SUBS, k % SUBS, rows], ident[:, :], is_transpose=True,
                                     start=False, stop=False, skip_group_check=True)
                    last = nc.tensor.matmul(acc, gated[:, k % SUBS, rows], w_o[:, :],
                                            start=False, stop=True, skip_group_check=True)
                last.then_inc(outputs, 1)

            def body(lap, k):
                output(lap, k)
                if exists(lap, k, AHEAD):
                    gate_product(*moved(lap, k, AHEAD))

            for k in range(AHEAD):
                gate_product(0, k)
            run_steps(pe, body)

        @block.scalar
        def _(act):
            act.wait_ge(consts_in, 16 * (5 + TILES))

            def sigmoid(lap, k):
                step = lap * BODY + k
                act.wait_ge(gate_sums, step + 1)
                nc.scalar.activation(ps_g[:, k % 2, :], ps_g[:, k % 2, :], ACT.Sigmoid,
                                     bias=bias_g[:, 0:1]).then_inc(gates, 1)

            def normalise(lap, k):
                batch = k // BATCH
                if k % BATCH == 0:
                    act.wait_ge(shifts, lap * BATCHES + (batch + 1))
                if k % SUBS == 0 and at_least(lap, k, BODY):
                    act.wait_ge(stored[k // SUBS], lap * 16)
                for t in range(TILES):
                    i = k % BATCH * TILES + t
                    last = nc.scalar.activation(o_step(k)[:, t, :], ps_o[:, k % BANKS, t, :], ACT.Identity,
                                                scale=scale[:, batch, ROOT_ROUNDS, i:i + 1],
                                                bias=shift[:, batch, i:i + 1])
                last.then_inc(normed, 1)

            def body(lap, k):
                if at_least(lap, k, NORM_LAG):
                    normalise(*moved(lap, k, -NORM_LAG))
                if exists(lap, k, AHEAD):
                    sigmoid(*moved(lap, k, AHEAD))

            for k in range(AHEAD):
                sigmoid(0, k)
            run_steps(act, body)
            for step in range(STEPS - NORM_LAG, STEPS):
                normalise(*moved(0, step, 0))

        @block.vector
        def _(dve):
            dve.wait_ge(consts_in, 16 * (5 + TILES))
            dve.wait_ge(consts_ready, 1)
            for i in range(3):
                nc.vector.tensor_copy(bo_part[:, i, :], bo_rest[:, :]).then_inc(bo_chain, 1)
                dve.wait_ge(bo_chain, 3 * i + 1)
                nc.vector.tensor_tensor(bo_rest[:, :], bo_rest[:, :], bo_part[:, i, :],
                                        ALU.subtract).then_inc(bo_chain, 1)
                if i == 0:
                    nc.vector.tensor_scalar(bo_sum[:, :], bo_part[:, 0, :], ident[0:3, 0:1], None,
                                            ALU.mult).then_inc(bo_chain, 1)
                else:
                    nc.vector.scalar_tensor_tensor(bo_sum[:, :], bo_part[:, i, :], ident[0:3, i:i + 1], bo_sum[:, :],
                                                   ALU.mult, ALU.add).then_inc(bo_chain, 1)
                dve.wait_ge(bo_chain, 3 * i + 3)
            nc.vector.tensor_copy(bo_split[:, :], bo_sum[:, :]).then_inc(consts_ready, 1)

            def gating(lap, k):
                step = lap * BODY + k
                slot, sub = k // SUBS, k % SUBS
                if sub == 0:
                    dve.wait_ge(u_in[slot], lap * 16 + 16)
                dve.wait_ge(gates, step + 1)
                if at_least(lap, k, SUBS):
                    dve.wait_ge(outputs, step - (SUBS - 1))
                nc.vector.tensor_tensor(gated[:, sub, :], ps_g[:, k % 2, :], u_t[:, slot, sub, :],
                                        ALU.mult).then_inc(gateds, 1)

            def statistics(lap, k, t):
                if t == 0:
                    dve.wait_ge(outputs, lap * BODY + (k + 1))
                return nc.vector.bn_stats(stats[:, k // BATCH, k % BATCH * TILES + t, :], ps_o[:, k % BANKS, t, :])


            def on_chain(lap, batch, count):
                dve.wait_ge(chain, lap * (CHAIN * BATCHES) + (CHAIN * batch + count))

            def differences(lap, b):
                on_chain(lap, b, 1)
                nc.vector.tensor_tensor(diff[:, b], stats[:, b, :, 1], stats[:, b, :, 4],
                                        ALU.subtract).then_inc(chain, 1)
                nc.vector.tensor_tensor(sums[:, b], stats[:, b, :, 1:3], stats[:, b, :, 4:6],
                                        ALU.add).then_inc(chain, 1)

            def squares(lap, b):
                on_chain(lap, b, 3)
                nc.vector.tensor_tensor(sqdiff[:, b], diff[:, b], diff[:, b], ALU.mult).then_inc(chain, 1)
                nc.vector.tensor_scalar(var_part[:, b], sums[:, b, :, 1], 4.0 / P, 4 * EPS,
                                        ALU.mult, ALU.add).then_inc(chain, 1)

            def variance(lap, b):
                on_chain(lap, b, 5)
                nc.vector.tensor_tensor(var[:, b], var_part[:, b], sqdiff[:, b], ALU.add).then_inc(chain, 1)

            def root_seed(lap, b):
                on_chain(lap, b, 6)
                nc.vector.tensor_scalar(scale[:, b, 0, :].bitcast(I32), var[:, b].bitcast(I32), -0.5, ROOT_SEED,
                                        ALU.mult, ALU.add).then_inc(chain, 1)

            def root_start(lap, b):
                on_chain(lap, b, 7)
                nc.vector.tensor_tensor(root[:, b, 0, :], var[:, b], scale[:, b, 0, :], ALU.mult).then_inc(chain, 1)

            def root_residual(lap, b, n):
                on_chain(lap, b, 8 + 3 * n)
                nc.vector.scalar_tensor_tensor(residual[:, b, n, :], root[:, b, n, :], -0.5, scale[:, b, n, :],
                                               ALU.mult, ALU.mult).then_inc(chain, 1)

            def root_update(lap, b, n):
                on_chain(lap, b, 9 + 3 * n)
                nc.vector.scalar_tensor_tensor(scale[:, b, n + 1, :], residual[:, b, n, :], 1.5, scale[:, b, n, :],
                                               ALU.add, ALU.mult).then_inc(chain, 1)
                if n + 1 < ROOT_ROUNDS:
                    nc.vector.scalar_tensor_tensor(root[:, b, n + 1, :], residual[:, b, n, :], 1.5, root[:, b, n, :],
                                                   ALU.add, ALU.mult).then_inc(chain, 1)

            def mean_shift(lap, b):
                on_chain(lap, b, CHAIN)
                nc.vector.scalar_tensor_tensor(shift[:, b], sums[:, b, :, 0], -0.5, scale[:, b, ROOT_ROUNDS, :],
                                               ALU.mult, ALU.mult).then_inc(shifts, 1)

            def add_beta(lap, k):
                dve.wait_ge(scaled, lap * BODY + (k + 1))
                tiles = o_step(k)[:, BETA_SPLIT:TILES, :]
                nc.vector.tensor_tensor(tiles, tiles,
                                        beta_b[:, :].unsqueeze(1).to_broadcast([P, TILES - BETA_SPLIT, P]),
                                        ALU.add).then_inc(finished_dve, 1)

            def gating_ahead(lap, k):
                if exists(lap, k, AHEAD):
                    gating(*moved(lap, k, AHEAD))

            def beta_behind(lap, k):
                if at_least(lap, k, BETA_LAG):
                    add_beta(*moved(lap, k, -BETA_LAG))

            def body(lap, k):
                old_lap, old_k = moved(lap, k, -BATCH)
                old = old_k // BATCH
                small = at_least(lap, k, BATCH)
                if k % BATCH == 0:
                    statistics(lap, k, 0)
                    if small:
                        root_start(old_lap, old)
                    statistics(lap, k, 1)
                    if small:
                        root_residual(old_lap, old, 0)
                    statistics(lap, k, 2)
                    if small:
                        root_update(old_lap, old, 0)
                    statistics(lap, k, 3)
                    if small:
                        root_residual(old_lap, old, 1)
                    gating_ahead(lap, k)
                    if small:
                        root_update(old_lap, old, 1)
                    beta_behind(lap, k)
                    if small:
                        root_residual(old_lap, old, 2)
                elif k % BATCH == 1:
                    statistics(lap, k, 0)
                    if small:
                        root_update(old_lap, old, 2)
                    statistics(lap, k, 1)
                    if small:
                        mean_shift(old_lap, old)
                    statistics(lap, k, 2)
                    statistics(lap, k, 3)
                    gating_ahead(lap, k)
                    beta_behind(lap, k)
                else:
                    for t in range(TILES):
                        last = statistics(lap, k, t)
                    last.then_inc(chain, 1)
                    gating_ahead(lap, k)
                    differences(lap, k // BATCH)
                    beta_behind(lap, k)
                    squares(lap, k // BATCH)
                    variance(lap, k // BATCH)
                    root_seed(lap, k // BATCH)

            for k in range(AHEAD):
                gating(0, k)
            for k in range(BODY):
                body(0, k)
            with dve.Fori(1, LOOPS) as lap:
                for k in range(BODY):
                    body(lap, k)
            for k in range(STEPS - LOOPS * BODY - 1):
                body(LOOPS, k)
            lap, k = moved(0, STEPS - 1, 0)
            b = k // BATCH
            old_lap, old_k = moved(lap, k, -BATCH)
            root_update(old_lap, old_k // BATCH, 2)
            mean_shift(old_lap, old_k // BATCH)
            for t in range(TILES):
                last = statistics(lap, k, t)
            last.then_inc(chain, 1)
            beta_behind(lap, k)
            differences(lap, b)
            squares(lap, b)
            variance(lap, b)
            root_seed(lap, b)
            root_start(lap, b)
            for n in range(ROOT_ROUNDS):
                root_residual(lap, b, n)
                root_update(lap, b, n)
            mean_shift(lap, b)
            for step in range(STEPS - BETA_LAG, STEPS):
                add_beta(*moved(0, step, 0))

        @block.gpsimd
        def _(pool):
            nc.gpsimd.memset(ident[:, :], 0.0).then_inc(setup, 1)
            nc.gpsimd.memset(ones3[:, :], 1.0).then_inc(setup, 1)
            pool.wait_ge(setup, 2)
            nc.gpsimd.affine_select(out=ident[:, :], in_=ident[:, :], compare_op=ALU.not_equal, fill=1.0, base=0,
                                    pattern=[[-1, P]], channel_multiplier=1).then_inc(consts_ready, 1)
            pool.wait_ge(consts_in, 16 * (5 + TILES))
            nc.gpsimd.tensor_scalar(gamma_b[:, :], gamma_b[:, :], 2.0, None, ALU.mult).then_inc(setup, 1)
            pool.wait_ge(setup, 3)

            def times_gamma(lap, k):
                pool.wait_ge(normed, lap * BODY + (k + 1))
                nc.gpsimd.tensor_tensor(o_step(k), o_step(k), gamma_b[:, :].unsqueeze(1).to_broadcast([P, TILES, P]),
                                        ALU.mult).then_inc(scaled, 1)

            def add_beta(lap, k):
                pool.wait_ge(scaled, lap * BODY + (k + 1))
                tiles = o_step(k)[:, 0:BETA_SPLIT, :]
                nc.gpsimd.tensor_tensor(tiles, tiles, beta_b[:, :].unsqueeze(1).to_broadcast([P, BETA_SPLIT, P]),
                                        ALU.add).then_inc(finished_pool, 1)

            def body(lap, k):
                if at_least(lap, k, GAMMA_LAG):
                    times_gamma(*moved(lap, k, -GAMMA_LAG))
                if at_least(lap, k, BETA_LAG):
                    add_beta(*moved(lap, k, -BETA_LAG))

            run_steps(pool, body)
            times_gamma(*moved(0, STEPS - GAMMA_LAG, 0))
            for step in range(STEPS - BETA_LAG, STEPS):
                if step + BETA_LAG - GAMMA_LAG + 1 < STEPS:
                    times_gamma(*moved(0, step + BETA_LAG - GAMMA_LAG + 1, 0))
                add_beta(*moved(0, step, 0))


def build(nc, xT, Wa, ba, Wb, bb, Wg, bg, Wo, bo, gamma, beta, out):
    ab_scratch = nc.dram_tensor("ab_scratch", [GROUPS, 2, COL_BLOCKS, ROW_TILES, P, RUN], F32, kind="Internal").ap()
    u_store = nc.dram_tensor("u_scratch", [P, N * N + PAD], F32, kind="Internal").ap()
    u_values = u_store[:, 0:N * N]
    project(nc, xT, Wa, Wb, ba, bb, ab_scratch)
    contract(nc, ab_scratch, u_values.rearrange("c (t k r) -> c t k r", t=ROW_TILES, k=N))
    finish(nc, xT, Wg, Wo, bg, bo, gamma, beta, u_values.rearrange("c (m f) -> c m f", m=CHUNKS), out)


_NAMES = ["L0_conv_Wa", "L0_conv_ba", "L0_conv_Wb", "L0_conv_bb", "L0_conv_Wg", "L0_conv_bg",
          "L0_conv_Wo", "L0_conv_bo", "L0_conv_gamma", "L0_conv_beta"]


def kernel(**inputs):
    import concourse.bacc as bacc
    from concourse.bass_utils import run_bass_kernel_spmd

    nc = bacc.Bacc("TRN2", target_bir_lowering=False, num_devices=1)
    x = np.asarray(inputs["x"])[0]
    blocks = N // CHUNK_COLS
    x = x.reshape(ROW_TILES, P, blocks, CHUNK_COLS, P).transpose(0, 2, 4, 3, 1)
    arrays = {"in_xT": np.ascontiguousarray(x).reshape(CHUNKS, P, CHUNK)}
    for name in _NAMES:
        arrays["in_" + name] = np.ascontiguousarray(inputs[name])
    args = [nc.dram_tensor(n, a.shape, mybir.dt.from_np(a.dtype), kind="ExternalInput").ap()
            for n, a in arrays.items()]
    out = nc.dram_tensor("out_dram", (CHUNKS, P, CHUNK), F32, kind="ExternalOutput").ap()
    build(nc, *args, out)
    r = run_bass_kernel_spmd(nc, [arrays], core_ids=[0])
    got = np.asarray(r.results[0]["out_dram"]).reshape(ROW_TILES, blocks, P, CHUNK_COLS, P)
    return np.ascontiguousarray(got.transpose(0, 2, 1, 3, 4)).reshape(1, N, N, P)
```

```python
from contextlib import ExitStack

import numpy as np
import concourse.bass as bass
from concourse import mybir
from concourse.alu_op_type import AluOpType as ALU

F32 = mybir.dt.float32
F32R = mybir.dt.float32r
I32 = mybir.dt.int32
BF16 = mybir.dt.bfloat16
ACT = mybir.ActivationFunctionType

P = 128
N = 512
ROW_TILES = N // P
COL_BLOCK = 64
COL_BLOCKS = N // COL_BLOCK
UNITS = COL_BLOCKS * ROW_TILES
CHUNK_COLS = 16
QUARTERS = COL_BLOCK // CHUNK_COLS
CHUNK = CHUNK_COLS * P
CHUNKS = N * N // CHUNK
GROUP = 4
GROUPS = P // GROUP
KEPT = 2
AB_STORES = 3
RUN = GROUP * COL_BLOCK
PAD = 1024
EPS = 1e-5


class FinishConstants:

    LOADS = 9

    def __init__(self, nc, ctx):
        sb = lambda name, shape, dt=F32: ctx.enter_context(nc.sbuf_tensor(name, shape, dt))
        self.w_g = sb("w_g", [P, P])
        self.w_o = sb("w_o", [P, P])
        self.ident = sb("ident", [P, P])
        self.bias_g = sb("bias_g", [P, 1])
        self.gamma_b = sb("gamma_b", [P, P])
        self.beta_b = sb("beta_b", [P, P])
        self.ones3 = sb("ones3", [3, P], BF16)
        self.bo_split = sb("bo_split", [3, N], BF16)
        self.bo_rest = sb("bo_rest", [3, N])
        self.bo_part = sb("bo_part", [3, 3, N], BF16)
        self.bo_sum = sb("bo_sum", [3, N])


class Shared:

    def __init__(self, nc, ctx):
        shape = [P, KEPT, ROW_TILES, N]

        def place(name, low_name):
            offset = nc.sbuf_base
            buffer = ctx.enter_context(nc.sbuf_tensor(name, shape, F32))
            return buffer, nc.alloc_sbuf_tensor_at(low_name, shape, F32R, offset=offset)

        self.kept_a, self.a_low = place("kept_a_u_out", "kept_a_low")
        self.kept_b, self.b_low = place("kept_b", "b_low")
        self.ab_stored = [ctx.enter_context(nc.semaphore(f"ab_stored{s}")) for s in range(2)]
        self.u_stored = [ctx.enter_context(nc.semaphore(f"u_stored{s}")) for s in range(2)]


def project(nc, xT, Wa, Wb, ba, bb, ab_scratch, shared, c, Wg, Wo, bg, bo, gamma, beta):
    PSUM_SLOTS = 4
    GCOLS = 4
    STEPS = COL_BLOCK // GCOLS
    QSTEPS = STEPS // QUARTERS
    stored = shared.ab_stored
    with ExitStack() as ctx:
        sb = lambda name, shape, dt=F32: ctx.enter_context(nc.sbuf_tensor(name, shape, dt))
        sem = lambda name: ctx.enter_context(nc.semaphore(name))
        w_ab = sb("w_ab", [P, 2 * P])
        bias_ab = sb("bias_ab", [P, 2 * P])
        x_tile = sb("x_tile", [P, QUARTERS, CHUNK_COLS, P])
        stage = sb("stage", [P, 2, 2 * P, COL_BLOCK])
        ps = ctx.enter_context(nc.psum_tensor("ps_ab", [P, PSUM_SLOTS, GCOLS, 2 * P], F32))
        weights_in = sem("p1_weights_in")
        bias_in = sem("p1_bias_in")
        x_in = [sem(f"p1_x_in{q}") for q in range(QUARTERS)]
        products = sem("p1_products")
        staged = sem("p1_staged")
        kept = sem("p1_kept")
        consts_in = sem("consts_in")
        setup = sem("consts_setup")
        identity_ready = sem("identity_ready")
        bo_chain = sem("bo_chain")
        block = ctx.enter_context(nc.Block())

        @block.sync
        def _(sp):
            sp.dma_start(w_ab[:, 0:P], Wa).then_inc(weights_in, 16)
            sp.dma_start(w_ab[:, P:2 * P], Wb).then_inc(weights_in, 16)

            def store(cb, jt, unit):
                sp.wait_ge(staged, STEPS * (unit + 1))
                for ab in range(2):
                    sp.dma_start(
                        ab_scratch[1:GROUPS, ab, cb, jt, :, :].rearrange("g p f -> p g f"),
                        stage[:, jt % 2, ab * P + GROUP:(ab + 1) * P, :].rearrange("p (g c) i -> p g (c i)", c=GROUP),
                    ).then_inc(stored[jt % 2], 16)
                sp.dma_start(
                    ab_scratch[0, :, cb, jt, :, KEPT * COL_BLOCK:].rearrange("a p f -> p a f"),
                    stage[:, jt % 2, :, :].rearrange("p (a c) i -> p a (c i)", a=2)[
                        :, :, KEPT * COL_BLOCK:GROUP * COL_BLOCK]).then_inc(stored[jt % 2], 16)

            def unit_step(cb, jt, first):
                unit = cb * ROW_TILES + jt
                for q in range(QUARTERS):
                    if not first:
                        sp.wait_ge(products, STEPS * (unit - 1) + QSTEPS * (q + 1))
                    sp.dma_start(x_tile[:, q, :, :].rearrange("p a b -> p (a b)"),
                                 xT[cb * QUARTERS + (jt * (N // CHUNK_COLS) + q), :, :]).then_inc(x_in[q], 16)
                if not first:
                    if jt:
                        store(cb, jt - 1, unit - 1)
                    else:
                        store(cb - 1, ROW_TILES - 1, unit - 1)

            for jt in range(ROW_TILES):
                unit_step(0, jt, jt == 0)
            with sp.Fori(1, COL_BLOCKS) as cb:
                for jt in range(ROW_TILES):
                    unit_step(cb, jt, False)
            store(COL_BLOCKS - 1, ROW_TILES - 1, UNITS - 1)

        @block.tensor
        def _(pe):
            pe.wait_ge(weights_in, 32)

            def unit_step(unit, primed):
                for q in range(QUARTERS):
                    pe.wait_ge(x_in[q], 16 * (unit + 1))
                    for g in range(QSTEPS):
                        step = unit * STEPS + (q * QSTEPS + g)
                        if primed or q:
                            pe.wait_ge(staged, step - (PSUM_SLOTS - 1))
                        for i in range(GCOLS):
                            last = nc.tensor.matmul(ps[:, g, i, :], x_tile[:, q, g * GCOLS + i, :], w_ab[:, :],
                                                    start=i % 2 == 0, stop=True, skip_group_check=True)
                        last.then_inc(products, 1)

            for jt in range(ROW_TILES):
                unit_step(jt, jt > 0)
            with pe.Fori(1, COL_BLOCKS) as cb:
                for jt in range(ROW_TILES):
                    unit_step(cb * ROW_TILES + jt, True)

        @block.scalar
        def _(act):
            act.dma_start(bias_ab[:, 0:P], ba[None, :].to_broadcast([P, P])).then_inc(bias_in, 16)
            act.dma_start(bias_ab[:, P:2 * P], bb[None, :].to_broadcast([P, P])).then_inc(bias_in, 16)
            act.dma_start(c.w_g[:, :], Wg).then_inc(consts_in, 16)
            act.dma_start(c.w_o[:, :], Wo).then_inc(consts_in, 16)
            act.dma_start(c.bias_g[:, :], bg[:, None]).then_inc(consts_in, 16)
            act.dma_start(c.gamma_b[:, :], gamma[None, :].to_broadcast([P, P])).then_inc(consts_in, 16)
            act.dma_start(c.beta_b[:, :], beta[None, :].to_broadcast([P, P])).then_inc(consts_in, 16)
            for t in range(N // P):
                act.dma_start(c.bo_rest[:, t * P:(t + 1) * P],
                              bo[None, :].to_broadcast([3, P])).then_inc(consts_in, 16)
            act.wait_ge(consts_in, 16 * c.LOADS)

            def keep(cb, jt):
                act.wait_ge(staged, (cb * ROW_TILES + (jt + 1)) * STEPS)
                for ab, target in enumerate((shared.kept_a, shared.kept_b)):
                    nc.scalar.activation(target[:, :, jt, bass.ds(cb * COL_BLOCK, COL_BLOCK)],
                                         stage[:, jt % 2, ab * P:ab * P + KEPT, :], ACT.Copy).then_inc(kept, 1)

            for jt in range(ROW_TILES):
                keep(0, jt)
            with act.Fori(1, COL_BLOCKS) as cb:
                for jt in range(ROW_TILES):
                    keep(cb, jt)

        @block.gpsimd
        def _(pool):
            nc.gpsimd.memset(c.ident[:, :], 0.0).then_inc(setup, 1)
            nc.gpsimd.memset(c.ones3[:, :], 1.0).then_inc(setup, 1)
            pool.wait_ge(setup, 2)
            nc.gpsimd.affine_select(out=c.ident[:, :], in_=c.ident[:, :], compare_op=ALU.not_equal, fill=1.0,
                                    base=0, pattern=[[-1, P]], channel_multiplier=1).then_inc(identity_ready, 1)

        @block.vector
        def _(dve):
            dve.wait_ge(bias_in, 32)

            def unit_step(unit, jt, primed):
                if primed:
                    dve.wait_ge(stored[jt % 2], 16 * AB_STORES // 2 * (unit - jt % 2))
                    dve.wait_ge(kept, 2 * (unit - 1))
                for s in range(STEPS):
                    dve.wait_ge(products, unit * STEPS + (s + 1))
                    nc.vector.tensor_tensor(
                        stage[:, jt % 2, :, s * GCOLS:(s + 1) * GCOLS],
                        ps[:, s % PSUM_SLOTS, :, :].rearrange("p i c -> p c i"),
                        bias_ab[:, :].unsqueeze(2).to_broadcast([P, 2 * P, GCOLS]), ALU.add).then_inc(staged, 1)

            def split_bo():
                dve.wait_ge(consts_in, 16 * c.LOADS)
                dve.wait_ge(identity_ready, 1)
                for i in range(3):
                    nc.vector.tensor_copy(c.bo_part[:, i, :], c.bo_rest[:, :]).then_inc(bo_chain, 1)
                    dve.wait_ge(bo_chain, 3 * i + 1)
                    nc.vector.tensor_tensor(c.bo_rest[:, :], c.bo_rest[:, :], c.bo_part[:, i, :],
                                            ALU.subtract).then_inc(bo_chain, 1)
                    if i == 0:
                        nc.vector.tensor_scalar(c.bo_sum[:, :], c.bo_part[:, 0, :], c.ident[0:3, 0:1], None,
                                                ALU.mult).then_inc(bo_chain, 1)
                    else:
                        nc.vector.scalar_tensor_tensor(c.bo_sum[:, :], c.bo_part[:, i, :], c.ident[0:3, i:i + 1],
                                                       c.bo_sum[:, :], ALU.mult, ALU.add).then_inc(bo_chain, 1)
                    dve.wait_ge(bo_chain, 3 * i + 3)
                nc.vector.tensor_copy(c.bo_split[:, :], c.bo_sum[:, :]).then_inc(bo_chain, 1)

            for jt in range(ROW_TILES):
                unit_step(jt, jt, jt >= 2)
            split_bo()
            with dve.Fori(1, COL_BLOCKS) as cb:
                for jt in range(ROW_TILES):
                    unit_step(cb * ROW_TILES + jt, jt, True)


def contract(nc, ab_scratch, shared, u_scratch):
    with ExitStack() as ctx:
        sb = lambda name, shape, dt=F32: ctx.enter_context(nc.sbuf_tensor(name, shape, dt))
        sem = lambda name: ctx.enter_context(nc.semaphore(name))
        high = sb("ab_high", [P, 2, 2, ROW_TILES, N], F32R)
        group_ab = sb("group_ab", [P, 2, 2, COL_BLOCKS, ROW_TILES, GROUP, COL_BLOCK], F32R)
        kept, kept_low = (shared.kept_a, shared.kept_b), (shared.a_low, shared.b_low)
        b_lows = shared.b_low
        u_out = shared.kept_a
        ps = ctx.enter_context(nc.psum_tensor("ps_u", [P, 2, ROW_TILES, N], F32))
        loaded = [sem(f"p2_loaded{s}") for s in range(2)]
        first_loaded = sem("p2_first_loaded")
        highs = sem("p2_highs")
        lows = sem("p2_lows")
        products = sem("p2_products")
        evacuated = sem("p2_evacuated")
        stored = shared.u_stored
        block = ctx.enter_context(nc.Block())

        def raw(group, slot, ab, c):
            if is_kept(group, c):
                return by_block(kept[ab][:, c])
            return group_ab[:, slot, ab, :, :, c, :].bitcast(F32)

        def is_kept(group, c):
            return isinstance(group, int) and group == 0 and c < KEPT

        def by_block(rows):
            return rows.rearrange("p t (b i) -> p b t i", i=COL_BLOCK)

        @block.sync
        def _(sp):
            def load(group, slot):
                for ab in range(2):
                    sp.dma_start(
                        group_ab[:, slot, ab].rearrange("p b t c i -> p (b t) (c i)").bitcast(F32),
                        ab_scratch[group, ab].rearrange("b t p f -> p (b t) f")).then_inc(loaded[slot], 16)

            def store(group, c):
                channel = group * GROUP + c
                sp.wait_ge(evacuated, channel + 1)
                for kt in range(ROW_TILES):
                    sp.dma_start(
                        u_scratch[channel, :, kt * P:(kt + 1) * P, :].rearrange("t k r -> k t r"),
                        u_out[:, c % 2, kt, :].rearrange("p (t r) -> p t r", r=P)).then_inc(stored[c % 2], 16)

            def group_step(group, slot, more):
                for c in range(GROUP):
                    store(group, c)
                if more:
                    sp.wait_ge(products, GROUP * (group + 1))
                    load(group + 2, slot)

            for s in range(2):
                sp.wait_ge(shared.ab_stored[s], 16 * AB_STORES * UNITS // 2)
            for ab in range(2):
                sp.dma_start(
                    group_ab[:, 0, ab, :, :, KEPT:, :].rearrange("p b t c i -> p (b t) (c i)").bitcast(F32),
                    ab_scratch[0, ab, :, :, :, KEPT * COL_BLOCK:].rearrange("b t p f -> p (b t) f")
                ).then_inc(first_loaded, 16)
            load(1, 1)
            with sp.Fori(0, GROUPS // 2 - 1) as it:
                for slot in range(2):
                    group_step(it * 2 + slot, slot, True)
            for slot in range(2):
                group_step(GROUPS - 2 + slot, slot, False)

        @block.scalar
        def _(act):
            def cut_high(group, slot, c, primed):
                if isinstance(group, int) and group == 0:
                    if c == KEPT:
                        act.wait_ge(first_loaded, 32)
                elif c == 0:
                    act.wait_ge(loaded[slot], 16 * group + 16 * slot)
                if primed:
                    act.wait_ge(products, group * GROUP + (c - 1))
                for ab in range(2):
                    nc.scalar.activation(by_block(high[:, c % 2, ab]), raw(group, slot, ab, c),
                                         ACT.Copy).then_inc(highs, 1)

            def evacuate(group, c, primed):
                act.wait_ge(products, group * GROUP + (c + 1))
                if primed:
                    act.wait_ge(stored[c % 2], 16 * ROW_TILES // 2 * (group * GROUP + c - c % 2))
                nc.scalar.activation(u_out[:, c % 2, :, :], ps[:, c % 2, :, :], ACT.Copy).then_inc(evacuated, 1)

            def group_step(group, slot, first, last):
                for c in range(GROUP):
                    evacuate(group, c, not (first and c < 2))
                    if c < 2:
                        cut_high(group, slot, c + 2, True)
                    elif not last:
                        cut_high(group + 1, 1 - slot, c - 2, True)

            cut_high(0, 0, 0, False)
            cut_high(0, 0, 1, False)
            for slot in range(2):
                group_step(slot, slot, slot == 0, False)
            with act.Fori(1, GROUPS // 2 - 1) as it:
                for slot in range(2):
                    group_step(it * 2 + slot, slot, False, False)
            for slot in range(2):
                group_step(GROUPS - 2 + slot, slot, False, slot == 1)

        @block.vector
        def _(dve):
            def cut_low(group, slot, c):
                channel = group * GROUP + c
                for ab in range(2):
                    dve.wait_ge(highs, channel * 2 + (ab + 1))
                    if ab:
                        low = by_block(b_lows[:, c % 2])
                    else:
                        low = by_block(kept_low[0][:, c]) if is_kept(group, c) else group_ab[:, slot, 0, :, :, c, :]
                    nc.vector.tensor_tensor(low, raw(group, slot, ab, c),
                                            by_block(high[:, c % 2, ab]).bitcast(F32), ALU.subtract).then_inc(lows, 1)

            for slot in range(2):
                for c in range(GROUP):
                    cut_low(slot, slot, c)
            with dve.Fori(1, GROUPS // 2) as it:
                for slot in range(2):
                    for c in range(GROUP):
                        cut_low(it * 2 + slot, slot, c)

        @block.tensor
        def _(pe):
            def channel_step(group, slot, c, primed):
                channel = group * GROUP + c
                pe.wait_ge(highs, channel * 2 + 2)
                if primed:
                    pe.wait_ge(evacuated, channel - 1)
                for kt in range(ROW_TILES):
                    columns = slice(kt * P, (kt + 1) * P)
                    acc = ps[:, c % 2, kt, :]
                    for jt in range(ROW_TILES):
                        nc.tensor.matmul(acc, high[:, c % 2, 1, jt, columns], high[:, c % 2, 0, jt, :],
                                         start=jt == 0, stop=False)
                    if kt == 0:
                        pe.wait_ge(lows, channel * 2 + 1)
                    for jt in range(ROW_TILES):
                        a_low = kept_low[0][:, c, jt, :] if is_kept(group, c) else group_ab[:, slot, 0, :, jt, c, :]
                        nc.tensor.matmul(acc, high[:, c % 2, 1, jt, columns], a_low, start=False, stop=False)
                    if kt == 0:
                        pe.wait_ge(lows, channel * 2 + 2)
                    for jt in range(ROW_TILES):
                        last = nc.tensor.matmul(acc, b_lows[:, c % 2, jt, columns], high[:, c % 2, 0, jt, :],
                                                start=False, stop=jt == ROW_TILES - 1)
                last.then_inc(products, 1)

            for slot in range(2):
                for c in range(GROUP):
                    channel_step(slot, slot, c, slot > 0 or c >= 2)
            with pe.Fori(1, GROUPS // 2) as it:
                for slot in range(2):
                    for c in range(GROUP):
                        channel_step(it * 2 + slot, slot, c, True)


def finish(nc, xT, c, shared, u_scratch, out):
    RING = 5
    TILES = 4
    SUBS = CHUNK_COLS // TILES
    STEPS = CHUNKS * SUBS
    BODY = RING * SUBS
    LOOPS = STEPS // BODY
    BANKS = 5
    AHEAD = 2
    BATCH = 2
    BATCH_TILES = BATCH * TILES
    BATCHES = BODY // BATCH
    ROOT_SEED = float(0x5F3759DF)
    CUBIC = 3.0 / 8.0
    CHAIN = 10
    NORM_LAG = 4
    with ExitStack() as ctx:
        sb = lambda name, shape, dt=F32: ctx.enter_context(nc.sbuf_tensor(name, shape, dt))
        sem = lambda name: ctx.enter_context(nc.semaphore(name))
        x_t = sb("x_t", [P, RING, SUBS, N])
        u_t = sb("u_t", [P, RING, SUBS, N])
        o_t = sb("o_t", [P, RING, CHUNK_COLS, P])
        gated = sb("gated", [P, SUBS, N])
        stats = sb("stats", [P, 2, BATCH_TILES, 6])
        scale = sb("scale", [P, 2, 3, BATCH_TILES])
        factor = sb("factor", [P, 2, BATCH_TILES])
        shift = sb("shift", [P, 2, BATCH_TILES])
        ps_small = ctx.enter_context(nc.psum_tensor("ps_small", [P, 2, 6, BATCH_TILES], F32))
        ps_g = ctx.enter_context(nc.psum_tensor("ps_g", [P, 2, N], F32))
        ps_o = ctx.enter_context(nc.psum_tensor("ps_o", [P, BANKS, TILES, P], F32))
        x_in = [sem(f"p3_x_in{s}") for s in range(RING)]
        u_in = [sem(f"p3_u_in{s}") for s in range(RING)]
        gate_sums = sem("p3_gate_sums")
        gates = sem("p3_gates")
        gateds = sem("p3_gateds")
        outputs = sem("p3_outputs")
        measured = sem("p3_measured")
        moments = sem("p3_moments")
        chain = sem("p3_chain")
        shifts = sem("p3_shifts")
        normed = sem("p3_normed")
        scaled = sem("p3_scaled")
        finished = sem("p3_finished")
        last_scaled = sem("p3_last_scaled")
        last_finished = sem("p3_last_finished")
        stored = [sem(f"p3_stored{s}") for s in range(RING)]
        block = ctx.enter_context(nc.Block())


        def moved(lap, k, by):
            return lap + (k + by) // BODY, (k + by) % BODY

        def at_least(lap, k, bound):
            return not isinstance(lap, int) or lap * BODY + k >= bound

        def exists(lap, k, ahead):
            return not isinstance(lap, int) or lap * BODY + k + ahead < STEPS

        def run_steps(engine, body):
            for k in range(BODY):
                body(0, k)
            with engine.Fori(1, LOOPS) as lap:
                for k in range(BODY):
                    body(lap, k)
            for k in range(STEPS - LOOPS * BODY):
                body(LOOPS, k)

        def by_row(vector, rows):
            return vector[:, :].unsqueeze(1).to_broadcast([P, rows, P])

        def o_step(k):
            return o_t[:, k // SUBS, k % SUBS * TILES:(k % SUBS + 1) * TILES, :]

        @block.sync
        def _(sp):
            def load_x(chunk, slot):
                sp.dma_start(x_t[:, slot].rearrange("p a b -> p (a b)"), xT[chunk]).then_inc(x_in[slot], 16)

            def load_u(chunk, slot):
                sp.dma_start(u_t[:, slot].rearrange("p a b -> p (a b)"),
                             u_scratch[:, chunk, :]).then_inc(u_in[slot], 16)

            def store(chunk, slot):
                sp.wait_ge(finished, chunk + 1)
                sp.dma_start(out[chunk], o_t[:, slot].rearrange("p a b -> p (a b)")).then_inc(stored[slot], 16)

            def reload(chunk, slot):
                sp.wait_ge(outputs, SUBS * (chunk + 1))
                load_x(chunk + RING, slot)
                load_u(chunk + RING, slot)

            load_x(0, 0)
            for s in range(2):
                sp.wait_ge(shared.u_stored[s], 16 * ROW_TILES * P // 2)
            load_u(0, 0)
            for chunk in range(1, RING):
                load_x(chunk, chunk)
                load_u(chunk, chunk)
            reload(0, 0)
            reload(1, 1)
            with sp.Fori(0, (CHUNKS - RING - 2) // RING) as lap:
                for slot in range(RING):
                    store(lap * RING + slot, slot)
                    reload(lap * RING + (slot + 2), (slot + 2) % RING)
            for chunk in range((CHUNKS - RING - 2) // RING * RING, CHUNKS - 1):
                store(chunk, chunk % RING)
                if chunk + 2 + RING < CHUNKS:
                    reload(chunk + 2, (chunk + 2) % RING)
            sp.wait_ge(last_finished, SUBS)
            slot = (CHUNKS - 1) % RING
            sp.dma_start(out[CHUNKS - 1], o_t[:, slot].rearrange("p a b -> p (a b)")).then_inc(stored[slot], 16)
            for slot in range(RING):
                sp.wait_ge(stored[slot], 16 * len(range(slot, CHUNKS, RING)))

        @block.tensor
        def _(pe):
            def gate_product(lap, k):
                step = lap * BODY + k
                if k % SUBS == 0:
                    pe.wait_ge(x_in[k // SUBS], lap * 16 + 16)
                if at_least(lap, k, 2):
                    pe.wait_ge(gateds, step - 1)
                nc.tensor.matmul(ps_g[:, k % 2, :], c.w_g[:, :], x_t[:, k // SUBS, k % SUBS, :],
                                 start=True, stop=True).then_inc(gate_sums, 1)

            def output(lap, k):
                step = lap * BODY + k
                bank = k % BANKS
                if at_least(lap, k, BANKS):
                    pe.wait_ge(normed, step - (BANKS - 1))
                pe.wait_ge(gateds, step + 1)
                rows = [slice(t * P, (t + 1) * P) for t in range(TILES)]
                for t in range(TILES):
                    nc.tensor.matmul(ps_o[:, bank, t, :], x_t[:, k // SUBS, k % SUBS, rows[t]], c.ident[:, :],
                                     is_transpose=True, start=t == 0, stop=False, skip_group_check=True)
                nc.tensor.matmul(ps_o[:, bank].rearrange("p t c -> p (t c)"), c.ones3[:, :], c.bo_split[:, :],
                                 start=False, stop=False, skip_group_check=True)
                for t in range(TILES):
                    last = nc.tensor.matmul(ps_o[:, bank, t, :], gated[:, k % SUBS, rows[t]], c.w_o[:, :],
                                            start=False, stop=True, skip_group_check=True)
                last.then_inc(outputs, 1)

            def body(lap, k):
                output(lap, k)
                if exists(lap, k, AHEAD):
                    gate_product(*moved(lap, k, AHEAD))

            for k in range(AHEAD):
                gate_product(0, k)
            run_steps(pe, body)

        @block.scalar
        def _(act):
            def sigmoid(lap, k):
                step = lap * BODY + k
                act.wait_ge(gate_sums, step + 1)
                nc.scalar.activation(ps_g[:, k % 2, :], ps_g[:, k % 2, :], ACT.Sigmoid,
                                     bias=c.bias_g[:, 0:1]).then_inc(gates, 1)

            def normalise(lap, k):
                batch = k // BATCH
                if k % BATCH == 0:
                    act.wait_ge(shifts, lap * BATCHES + (batch + 1))
                if k % SUBS == 0 and at_least(lap, k, BODY):
                    act.wait_ge(stored[k // SUBS], lap * 16)
                for t in range(TILES):
                    i = k % BATCH * TILES + t
                    last = nc.scalar.activation(o_step(k)[:, t, :], ps_o[:, k % BANKS, t, :], ACT.Identity,
                                                scale=scale[:, batch % 2, 2, i:i + 1],
                                                bias=shift[:, batch % 2, i:i + 1])
                last.then_inc(normed, 1)

            def body(lap, k):
                if at_least(lap, k, NORM_LAG):
                    normalise(*moved(lap, k, -NORM_LAG))
                if exists(lap, k, AHEAD):
                    sigmoid(*moved(lap, k, AHEAD))

            for k in range(AHEAD):
                sigmoid(0, k)
            run_steps(act, body)
            for step in range(STEPS - NORM_LAG, STEPS):
                normalise(*moved(0, step, 0))

        @block.vector
        def _(dve):
            def gating(lap, k):
                step = lap * BODY + k
                slot, sub = k // SUBS, k % SUBS
                if sub == 0:
                    dve.wait_ge(u_in[slot], lap * 16 + 16)
                dve.wait_ge(gates, step + 1)
                nc.vector.tensor_tensor(gated[:, sub, :], ps_g[:, k % 2, :], u_t[:, slot, sub, :],
                                        ALU.mult).then_inc(gateds, 1)

            def statistics(lap, k, t):
                if t == 0:
                    dve.wait_ge(outputs, lap * BODY + (k + 1))
                nc.vector.bn_stats(stats[:, k // BATCH % 2, k % BATCH * TILES + t, :],
                                   ps_o[:, k % BANKS, t, :]).then_inc(measured, 1)

            def moment(lap, k, t):
                i = k % BATCH * TILES + t
                nc.vector.bn_aggr(ps_small[:, k // BATCH % 2, 0:2, i],
                                  stats[:, k // BATCH % 2, i, :]).then_inc(moments, 1)

            def all_measured(lap, k):
                dve.wait_ge(measured, (lap * BODY + (k + 1)) * TILES)


            def small(b):
                return [ps_small[:, b % 2, n, :] for n in range(6)]

            def on_chain(lap, b, count):
                dve.wait_ge(chain, lap * (CHAIN * BATCHES) + (CHAIN * b + count))

            def variance(lap, b):
                _, var, v, _, _, _ = small(b)
                dve.wait_ge(moments, lap * (BODY * TILES) + (b + 1) * BATCH_TILES)
                nc.vector.tensor_scalar(v, var, EPS, None, ALU.add).then_inc(chain, 1)

            def root_seed(lap, b):
                _, _, v, _, _, _ = small(b)
                on_chain(lap, b, 1)
                nc.vector.tensor_scalar(scale[:, b % 2, 0, :].bitcast(I32), v.bitcast(I32), -0.5, ROOT_SEED,
                                        ALU.mult, ALU.add).then_inc(chain, 1)

            def cubic_product(lap, b):
                _, _, v, product, _, _ = small(b)
                on_chain(lap, b, 2)
                nc.vector.tensor_tensor(product, v, scale[:, b % 2, 0, :], ALU.mult).then_inc(chain, 1)

            def cubic_h(lap, b):
                _, _, _, product, h, _ = small(b)
                on_chain(lap, b, 3)
                nc.vector.tensor_tensor(h, product, scale[:, b % 2, 0, :], ALU.mult).then_inc(chain, 1)

            def cubic_factor(lap, b):
                _, _, _, _, h, _ = small(b)
                on_chain(lap, b, 4)
                nc.vector.scalar_tensor_tensor(factor[:, b % 2], h, -10.0 / 3.0, scale[:, b % 2, 0, :],
                                               ALU.add, ALU.mult).then_inc(chain, 1)

            def cubic_term(lap, b):
                _, _, _, _, h, term = small(b)
                on_chain(lap, b, 5)
                nc.vector.tensor_tensor(term, h, factor[:, b % 2], ALU.mult).then_inc(chain, 1)

            def cubic_update(lap, b):
                _, _, _, _, _, term = small(b)
                on_chain(lap, b, 6)
                nc.vector.scalar_tensor_tensor(scale[:, b % 2, 1, :], scale[:, b % 2, 0, :], 5.0, term,
                                               ALU.mult, ALU.add).then_inc(chain, 1)

            def newton_product(lap, b):
                _, _, v, product, _, _ = small(b)
                on_chain(lap, b, 7)
                nc.vector.tensor_tensor(product, v, scale[:, b % 2, 1, :], ALU.mult).then_inc(chain, 1)

            def newton_term(lap, b):
                _, _, _, product, _, term = small(b)
                on_chain(lap, b, 8)
                nc.vector.scalar_tensor_tensor(term, product, -0.5 * CUBIC ** 3, scale[:, b % 2, 1, :],
                                               ALU.mult, ALU.mult).then_inc(chain, 1)

            def newton_update(lap, b):
                _, _, _, _, _, term = small(b)
                on_chain(lap, b, 9)
                nc.vector.scalar_tensor_tensor(scale[:, b % 2, 2, :], term, 1.5 * CUBIC, scale[:, b % 2, 1, :],
                                               ALU.add, ALU.mult).then_inc(chain, 1)

            def mean_shift(lap, b):
                mean, _, _, _, _, _ = small(b)
                on_chain(lap, b, CHAIN)
                nc.vector.scalar_tensor_tensor(shift[:, b % 2], mean, -1.0, scale[:, b % 2, 2, :],
                                               ALU.mult, ALU.mult).then_inc(shifts, 1)

            def gating_ahead(lap, k):
                if exists(lap, k, AHEAD):
                    gating(*moved(lap, k, AHEAD))

            def body(lap, k):
                old_lap, old_k = moved(lap, k, -BATCH)
                old = old_k // BATCH

                def small_step(operation):
                    if at_least(lap, k, BATCH):
                        operation(old_lap, old)

                if k % BATCH == 0:
                    statistics(lap, k, 0)
                    small_step(variance)
                    statistics(lap, k, 1)
                    small_step(root_seed)
                    statistics(lap, k, 2)
                    small_step(cubic_product)
                    statistics(lap, k, 3)
                    small_step(cubic_h)
                    all_measured(lap, k)
                    gating_ahead(lap, k)
                    small_step(cubic_factor)
                    moment(lap, k, 0)
                    small_step(cubic_term)
                    moment(lap, k, 1)
                    moment(lap, k, 2)
                    small_step(cubic_update)
                    moment(lap, k, 3)
                else:
                    small_step(newton_product)
                    statistics(lap, k, 0)
                    small_step(newton_term)
                    statistics(lap, k, 1)
                    small_step(newton_update)
                    statistics(lap, k, 2)
                    small_step(mean_shift)
                    statistics(lap, k, 3)
                    all_measured(lap, k)
                    gating_ahead(lap, k)
                    for t in range(TILES):
                        moment(lap, k, t)

            for k in range(AHEAD):
                gating(0, k)
            run_steps(dve, body)
            lap, k = moved(0, STEPS - 1, 0)
            dve.wait_ge(normed, STEPS - 2 * BATCH)
            for operation in (variance, root_seed, cubic_product, cubic_h, cubic_factor, cubic_term, cubic_update,
                              newton_product, newton_term, newton_update, mean_shift):
                operation(lap, k // BATCH)
            for step in range(STEPS - SUBS, STEPS):
                _, place = moved(0, step, 0)
                dve.wait_ge(normed, step + 1)
                nc.vector.tensor_tensor(o_step(place), o_step(place), by_row(c.gamma_b, TILES),
                                        ALU.mult).then_inc(last_scaled, 1)
                dve.wait_ge(last_scaled, step - (STEPS - SUBS) + 1)
                nc.vector.tensor_tensor(o_step(place), o_step(place), by_row(c.beta_b, TILES),
                                        ALU.add).then_inc(last_finished, 1)

        @block.gpsimd
        def _(pool):
            def affine(lap, k):
                slot = k // SUBS
                tiles = o_t[:, slot, :, :]
                pool.wait_ge(normed, lap * BODY + (slot + 1) * SUBS)
                nc.gpsimd.tensor_tensor(tiles, tiles, by_row(c.gamma_b, CHUNK_COLS),
                                        ALU.mult).then_inc(scaled, 1)
                pool.wait_ge(scaled, lap * RING + (slot + 1))
                nc.gpsimd.tensor_tensor(tiles, tiles, by_row(c.beta_b, CHUNK_COLS),
                                        ALU.add).then_inc(finished, 1)

            for slot in range(RING):
                affine(0, slot * SUBS)
            with pool.Fori(1, LOOPS) as lap:
                for slot in range(RING):
                    affine(lap, slot * SUBS)
            for slot in range(CHUNKS - LOOPS * RING - 1):
                affine(LOOPS, slot * SUBS)


def build(nc, xT, Wa, ba, Wb, bb, Wg, bg, Wo, bo, gamma, beta, out):
    ab_scratch = nc.dram_tensor("ab_scratch", [GROUPS, 2, COL_BLOCKS, ROW_TILES, P, RUN], F32, kind="Internal").ap()
    u_store = nc.dram_tensor("u_scratch", [P, N * N + PAD], F32, kind="Internal").ap()
    u_values = u_store[:, 0:N * N]
    ctx = ExitStack()
    with ctx:
        c = FinishConstants(nc, ctx)
        with ExitStack() as early:
            shared = Shared(nc, early)
            project(nc, xT, Wa, Wb, ba, bb, ab_scratch, shared, c, Wg, Wo, bg, bo, gamma, beta)
            contract(nc, ab_scratch, shared, u_values.rearrange("c (t k r) -> c t k r", t=ROW_TILES, k=N))
            finish(nc, xT, c, shared, u_values.rearrange("c (m f) -> c m f", m=CHUNKS), out)


_NAMES = ["L0_conv_Wa", "L0_conv_ba", "L0_conv_Wb", "L0_conv_bb", "L0_conv_Wg", "L0_conv_bg",
          "L0_conv_Wo", "L0_conv_bo", "L0_conv_gamma", "L0_conv_beta"]


def kernel(**inputs):
    import concourse.bacc as bacc
    from concourse.bass_utils import run_bass_kernel_spmd

    nc = bacc.Bacc("TRN2", target_bir_lowering=False, num_devices=1)
    x = np.asarray(inputs["x"])[0]
    blocks = N // CHUNK_COLS
    x = x.reshape(ROW_TILES, P, blocks, CHUNK_COLS, P).transpose(0, 2, 4, 3, 1)
    arrays = {"in_xT": np.ascontiguousarray(x).reshape(CHUNKS, P, CHUNK)}
    for name in _NAMES:
        arrays["in_" + name] = np.ascontiguousarray(inputs[name])
    args = [nc.dram_tensor(n, a.shape, mybir.dt.from_np(a.dtype), kind="ExternalInput").ap()
            for n, a in arrays.items()]
    out = nc.dram_tensor("out_dram", (CHUNKS, P, CHUNK), F32, kind="ExternalOutput").ap()
    build(nc, *args, out)
    r = run_bass_kernel_spmd(nc, [arrays], core_ids=[0])
    got = np.asarray(r.results[0]["out_dram"]).reshape(ROW_TILES, blocks, P, CHUNK_COLS, P)
    return np.ascontiguousarray(got.transpose(0, 2, 1, 3, 4)).reshape(1, N, N, P)
```
